# Optimizing a Trainium2 kernel written in Bass

```python
import numpy as np
import jax
import jax.numpy as jnp

def _softmax(x, axis=-1):
    return jax.nn.softmax(x, axis=axis)

def _gelu(x):
    return jax.nn.gelu(x, approximate=True)

def _silu(x):
    return jax.nn.silu(x)

def _sigmoid(x):
    return jax.nn.sigmoid(x)

def _layernorm(x, axis=-1, eps=1e-05):
    m = jnp.mean(x, axis=axis, keepdims=True)
    v = jnp.var(x, axis=axis, keepdims=True)
    return (x - m) / jnp.sqrt(v + eps)

def _scatter_add(tgt, idx, src, axis=0):
    return tgt.at[idx].add(src)

def _segment_sum(src, seg, n):
    return jax.ops.segment_sum(src, seg, n)
kernel_name = 'mk_adj_ffn_d1_adj_r2_55d0ba'

def setup_inputs(seed: int=0):
    np.random.seed(seed)
    _w = jnp.asarray

    def _rec_inputs():
        import jax
        import jax.numpy as jnp
        _gk = jax.random.key(seed)
        x = -0.0002928 + 1 * jax.random.normal(jax.random.fold_in(_gk, 1), (4096, 256), jnp.float32)
        _w = (1.0 + jnp.arange(4096, dtype=jnp.float32)) ** (-0.5)
        _w = _w / _w.mean()
        _pij = jnp.clip(0.00390625 * _w[:, None] * _w[None, :], 0.0, 1.0)
        _a = jax.random.uniform(jax.random.fold_in(_gk, 2), (4096, 4096)) < _pij
        _a = jnp.logical_or(_a, jnp.eye(4096, dtype=bool))
        _af = _a.astype(jnp.float32)
        _af = _af * jax.random.uniform(jax.random.fold_in(_gk, 3), (4096, 4096), jnp.float32, 0.05, 1)
        adj = _af
        return (x, adj)
    x, adj = _rec_inputs()

    def _L0_gnn_setup():
        import jax, jax.numpy as jnp
        import numpy as np
        N = 4096
        D_IN = 256
        D_OUT = 256
        key = jax.random.key(seed)
        k1, k2, k3, k4 = jax.random.split(key, 4)
        x = jax.random.normal(k1, (N, D_IN), dtype=jnp.float32)
        adj = jax.random.uniform(k2, (N, N), dtype=jnp.float32)
        bound = 1.0 / np.sqrt(D_IN)
        W = jax.random.uniform(k3, (D_OUT, D_IN), minval=-bound, maxval=bound, dtype=jnp.float32)
        b = jax.random.uniform(k4, (D_OUT,), minval=-bound, maxval=bound, dtype=jnp.float32)
        return {'x': x, 'adj': adj, 'W': W, 'b': b}
    _L0_gnn_all = _L0_gnn_setup()
    _L0_gnn_in = {k: v for k, v in _L0_gnn_all.items() if k in ('W', 'b')}
    del _L0_gnn_all

    def _L0_ffn_setup():
        import jax, jax.numpy as jnp
        import numpy as np
        D_MODEL, D_STATE, D_CONV, D_INPUT, D_OUTPUT = (512, 16, 4, 256, 256)
        EXPAND = 2
        D_INNER = EXPAND * D_MODEL
        DT_RANK = (D_MODEL + 15) // 16
        B, L = (4, 1024)

        def _mamba(x, W_in, conv_w, conv_b, W_xproj, W_dt, b_dt, A_log, Dp, W_out):
            xz = jnp.einsum('bld,ed->ble', x, W_in)
            u, z = jnp.split(xz, 2, axis=-1)
            u_pad = jnp.pad(u, ((0, 0), (D_CONV - 1, 0), (0, 0)))
            u = sum((u_pad[:, k:k + u.shape[1], :] * conv_w[:, k] for k in range(D_CONV))) + conv_b
            u = jax.nn.silu(u)
            dbc = jnp.einsum('bld,ed->ble', u, W_xproj)
            dt, B_ssm, C_ssm = jnp.split(dbc, [DT_RANK, DT_RANK + D_STATE], axis=-1)
            delta = jax.nn.softplus(jnp.einsum('blr,dr->bld', dt, W_dt) + b_dt)
            A = -jnp.exp(A_log)

            def step(h, ins):
                d_t, B_t, C_t, u_t = ins
                dA = jnp.exp(d_t[..., None] * A)
                h = dA * h + (d_t * u_t)[..., None] * B_t[:, None, :]
                y_t = jnp.einsum('bds,bs->bd', h, C_t)
                return (h, y_t)
            h0 = jnp.zeros((u.shape[0], D_INNER, D_STATE), u.dtype)
            xs = (delta.transpose(1, 0, 2), B_ssm.transpose(1, 0, 2), C_ssm.transpose(1, 0, 2), u.transpose(1, 0, 2))
            _, y = jax.lax.scan(step, h0, xs)
            y = y.transpose(1, 0, 2) + u * Dp
            y = y * jax.nn.silu(z)
            return jnp.einsum('bld,ed->ble', y, W_out)
        key = jax.random.key(seed)
        ks = jax.random.split(key, 16)
        s = lambda fan_in: 1.0 / np.sqrt(fan_in)
        inp = {'x': jax.random.normal(ks[0], (B, L, D_INPUT), jnp.float32), 'W_fc1': jax.random.normal(ks[1], (D_MODEL, D_INPUT), jnp.float32) * s(D_INPUT), 'b_fc1': jnp.zeros((D_MODEL,), jnp.float32), 'W_in': jax.random.normal(ks[2], (2 * D_INNER, D_MODEL), jnp.float32) * s(D_MODEL), 'conv_w': jax.random.normal(ks[3], (D_INNER, D_CONV), jnp.float32) * s(D_CONV), 'conv_b': jnp.zeros((D_INNER,), jnp.float32), 'W_xproj': jax.random.normal(ks[4], (DT_RANK + 2 * D_STATE, D_INNER), jnp.float32) * s(D_INNER), 'W_dt': jax.random.normal(ks[5], (D_INNER, DT_RANK), jnp.float32) * s(DT_RANK), 'b_dt': jax.random.uniform(ks[6], (D_INNER,), jnp.float32, -4.0, -2.0), 'A_log': jnp.log(jnp.broadcast_to(jnp.arange(1, D_STATE + 1, dtype=jnp.float32), (D_INNER, D_STATE))), 'D': jnp.ones((D_INNER,), jnp.float32), 'W_out': jax.random.normal(ks[7], (D_MODEL, D_INNER), jnp.float32) * s(D_INNER), 'W_fc2': jax.random.normal(ks[8], (D_OUTPUT, D_MODEL), jnp.float32) * s(D_MODEL), 'b_fc2': jnp.zeros((D_OUTPUT,), jnp.float32)}
        return inp
    _L0_ffn_all = _L0_ffn_setup()
    _L0_ffn_in = {k: v for k, v in _L0_ffn_all.items() if k in ('W_fc1', 'b_fc1', 'W_in', 'conv_w', 'conv_b', 'W_xproj', 'W_dt', 'b_dt', 'A_log', 'D', 'W_out', 'W_fc2', 'b_fc2')}
    del _L0_ffn_all
    return {'x': x, 'adj': adj, 'L0_gnn_W': _L0_gnn_in['W'], 'L0_gnn_b': _L0_gnn_in['b'], 'L0_ffn_W_fc1': _L0_ffn_in['W_fc1'], 'L0_ffn_b_fc1': _L0_ffn_in['b_fc1'], 'L0_ffn_W_in': _L0_ffn_in['W_in'], 'L0_ffn_conv_w': _L0_ffn_in['conv_w'], 'L0_ffn_conv_b': _L0_ffn_in['conv_b'], 'L0_ffn_W_xproj': _L0_ffn_in['W_xproj'], 'L0_ffn_W_dt': _L0_ffn_in['W_dt'], 'L0_ffn_b_dt': _L0_ffn_in['b_dt'], 'L0_ffn_A_log': _L0_ffn_in['A_log'], 'L0_ffn_D': _L0_ffn_in['D'], 'L0_ffn_W_out': _L0_ffn_in['W_out'], 'L0_ffn_W_fc2': _L0_ffn_in['W_fc2'], 'L0_ffn_b_fc2': _L0_ffn_in['b_fc2']}

def reference(x, adj, L0_gnn_W, L0_gnn_b, L0_ffn_W_fc1, L0_ffn_b_fc1, L0_ffn_W_in, L0_ffn_conv_w, L0_ffn_conv_b, L0_ffn_W_xproj, L0_ffn_W_dt, L0_ffn_b_dt, L0_ffn_A_log, L0_ffn_D, L0_ffn_W_out, L0_ffn_W_fc2, L0_ffn_b_fc2):
    import jax
    import jax.numpy as jnp

    def _L0_gnn_ref(x, adj, W, b):
        import jax, jax.numpy as jnp
        import numpy as np
        N = 4096
        D_IN = 256
        D_OUT = 256
        a = adj + jnp.eye(adj.shape[0], dtype=adj.dtype)
        d = jnp.sum(a, axis=1) ** (-0.5)
        a_norm = d[:, None] * a * d[None, :]
        support = a_norm @ x
        out = support @ W.T + b
        out = jax.nn.relu(out)
        return out

    def _L0_ffn_ref(x, W_fc1, b_fc1, W_in, conv_w, conv_b, W_xproj, W_dt, b_dt, A_log, D, W_out, W_fc2, b_fc2):
        import jax, jax.numpy as jnp
        import numpy as np
        D_MODEL, D_STATE, D_CONV, D_INPUT, D_OUTPUT = (512, 16, 4, 256, 256)
        EXPAND = 2
        D_INNER = EXPAND * D_MODEL
        DT_RANK = (D_MODEL + 15) // 16
        B, L = (4, 1024)

        def _mamba(x, W_in, conv_w, conv_b, W_xproj, W_dt, b_dt, A_log, Dp, W_out):
            xz = jnp.einsum('bld,ed->ble', x, W_in)
            u, z = jnp.split(xz, 2, axis=-1)
            u_pad = jnp.pad(u, ((0, 0), (D_CONV - 1, 0), (0, 0)))
            u = sum((u_pad[:, k:k + u.shape[1], :] * conv_w[:, k] for k in range(D_CONV))) + conv_b
            u = jax.nn.silu(u)
            dbc = jnp.einsum('bld,ed->ble', u, W_xproj)
            dt, B_ssm, C_ssm = jnp.split(dbc, [DT_RANK, DT_RANK + D_STATE], axis=-1)
            delta = jax.nn.softplus(jnp.einsum('blr,dr->bld', dt, W_dt) + b_dt)
            A = -jnp.exp(A_log)

            def step(h, ins):
                d_t, B_t, C_t, u_t = ins
                dA = jnp.exp(d_t[..., None] * A)
                h = dA * h + (d_t * u_t)[..., None] * B_t[:, None, :]
                y_t = jnp.einsum('bds,bs->bd', h, C_t)
                return (h, y_t)
            h0 = jnp.zeros((u.shape[0], D_INNER, D_STATE), u.dtype)
            xs = (delta.transpose(1, 0, 2), B_ssm.transpose(1, 0, 2), C_ssm.transpose(1, 0, 2), u.transpose(1, 0, 2))
            _, y = jax.lax.scan(step, h0, xs)
            y = y.transpose(1, 0, 2) + u * Dp
            y = y * jax.nn.silu(z)
            return jnp.einsum('bld,ed->ble', y, W_out)
        h = jnp.einsum('bli,oi->blo', x, W_fc1) + b_fc1
        h = _mamba(h, W_in, conv_w, conv_b, W_xproj, W_dt, b_dt, A_log, D, W_out)
        return jnp.einsum('bld,od->blo', h, W_fc2) + b_fc2
    x = x + _L0_gnn_ref(_layernorm(x, axis=-1), adj, L0_gnn_W, L0_gnn_b)
    x = x + _L0_ffn_ref(_layernorm(x, axis=-1)[None], L0_ffn_W_fc1, L0_ffn_b_fc1, L0_ffn_W_in, L0_ffn_conv_w, L0_ffn_conv_b, L0_ffn_W_xproj, L0_ffn_W_dt, L0_ffn_b_dt, L0_ffn_A_log, L0_ffn_D, L0_ffn_W_out, L0_ffn_W_fc2, L0_ffn_b_fc2)[0]
    return x

_drawn_inputs = setup_inputs


def setup_inputs(seed=0):
    import zlib

    import numpy as np

    out = dict(_drawn_inputs(seed))
    spreads = {'L0_ffn_b_fc1': (0.0, 0.1),
     'L0_ffn_conv_b': (0.0, 0.1),
     'L0_ffn_D': (1.0, 0.2),
     'L0_ffn_b_fc2': (0.0, 0.1)}
    factors = {}
    for name, (base, spread) in spreads.items():
        noise = np.random.default_rng([zlib.crc32(name.encode()), seed]).standard_normal(out[name].shape)
        drawn = base * np.exp(spread * noise) if base else spread * noise
        out[name] = jnp.asarray(drawn.astype(out[name].dtype))
    for name, factor in factors.items():
        out[name] = (out[name] * factor).astype(out[name].dtype)
    return out
```

```python
from contextlib import ExitStack

import numpy as np

import concourse.bass as bass
from concourse import mybir

F32 = mybir.dt.float32
ACT = mybir.ActivationFunctionType
ALU = mybir.AluOpType
AX_X = mybir.AxisListType.X

P = 128
N = 4096
C = 256
DM = 512
DI = 1024
NS = 16
R = 32
T = 512
NCH = N // T
TB = T // P
CT = DI // P
G = 4
NG = CT // G
FT = C // P
KT = DM // P
NJ = N // P
STEPS = NS + 1
EPS = 1e-5
PAIRS = NJ // 2
ADJ_SLOTS = 4
DEC_SLOTS = 4
DRV_SLOTS = 4
B_SLOTS = 4
FREE = 2


class Tally:

    def __init__(self, per=0):
        self.per, self.n, self.base = per, 0, 0

    def next(self):
        self.n += 1
        return self.base + self.n

    def value(self):
        return self.base + self.n

    def enter(self, k):
        self.start, self.base = self.n, k * self.per

    def leave(self, times):
        assert self.n - self.start == self.per, (self.n - self.start, self.per)
        self.n, self.base = self.start + times * self.per, 0


UNITS = NG * NS * G
SCAN_FREE = DEC_SLOTS
DRIVE_FREE = B_SLOTS * G

A_PER = 2 + CT + CT + 1 + 1 + CT + CT
D_GROUP = TB + TB // 2
D_PER = 2 + NG * D_GROUP
T_PER = NG * STEPS * TB


def build(nc, t):
    nc.disable_value_cache = True
    ctx = ExitStack()
    with ctx:
        def sb(name, *shape):
            return ctx.enter_context(nc.sbuf_tensor(name, [P, *shape], F32))

        def sem(name):
            return ctx.enter_context(nc.semaphore(name))

        xw_dram = nc.dram_tensor("xw_scratch", [N, C], F32, kind="Internal").ap()
        b_dram = nc.dram_tensor("b_scratch", [NCH, NS, T], F32, kind="Internal").ap()

        win_c = sb("win_c", FT, 2 * DI)
        wout_c = sb("wout_c", CT, C)
        wx = sb("wx", CT, P)
        wdt = sb("wdt", DI)
        diag = sb("diag", CT, 4, P)
        ident = sb("ident", P)
        bin_c = sb("bin_c", 2 * CT)
        convw = sb("convw", CT, 4)
        convb = sb("convb", CT)
        bdt = sb("bdt", CT)
        dpar = sb("dpar", CT)
        amat = sb("amat", CT, NS)
        gnn_b = sb("gnn_b", C)
        fc2_b = sb("fc2_b", C)
        mhalf = sb("mhalf", TB)
        dinv = sb("dinv", NJ)
        adj_r = sb("adj_r", ADJ_SLOTS, 2, T)
        xw_r = sb("xw_r", ADJ_SLOTS, 2, C)
        xin = sb("xin", TB, C)
        xwi = sb("xwi", TB, C)
        x1 = sb("x1", TB, C)
        mv = sb("mv", TB, 2)
        st = sb("st", TB, 6)
        rstd = sb("rstd", TB)
        xlnT = sb("xlnT", FT, T)
        upre = sb("upre", 2, T + 3)
        hist = sb("hist", CT, 3)
        dbc = sb("dbc", T)
        ccol = sb("ccol", NCH * TB, NS)
        bcast = sb("bcast", B_SLOTS, T)
        state = sb("state", NS, CT)
        yT = sb("yT", TB, G * P)
        big = sb("big", 14336)
        u = big[:, 0:4096].rearrange("p (i t) -> p i t", t=T)
        hbuf = big[:, 4096:8192].rearrange("p (b q t) -> p b q t", b=2, t=T)
        decay = big[:, 8192:10240].rearrange("p (b t) -> p b t", t=T)
        du = big[:, 10240:14336].rearrange("p (i t) -> p i t", t=T)
        big2 = sb("big2", 8192)
        delta = big2[:, 0:4096].rearrange("p (i t) -> p i t", t=T)
        zs = big2[:, 4096:6144].rearrange("p (q t) -> p q t", t=T)
        drive = big2[:, 6144:8192].rearrange("p (b t) -> p b t", t=T)
        winT = big[:, 0:8192].rearrange("p (m e) -> p m e", m=KT)
        woutM = big[:, 8192:12288].rearrange("p (m d) -> p m d", m=KT)
        wfc1 = big[:, 12288:13312].rearrange("p (m f) -> p m f", m=KT)
        wfc2T = big[:, 13312:14336].rearrange("p (m o) -> p m o", m=KT)
        gnn_w = yT[:, 0, :].rearrange("p (f o) -> p f o", f=FT)
        bfc1 = yT[:, 1, 0:KT]
        rows = big2[:, :].rearrange("p (b n) -> p b n", b=2)
        xj = xin[:, 0:2, :]
        xws = x1[:, 0:2, :]
        xnT = xwi[:, 0:2, :]
        stat = sb("stat", 2, 2)
        srstd = sb("srstd", 2)
        gT = upre[:, :, 0:T]

        def bank(name):
            return ctx.enter_context(nc.psum_tensor(name, [P, 512], F32))
        bank_a = [bank(f"bank_a{i}") for i in range(2)]
        bank_d = [bank(f"bank_d{i}") for i in range(2)]
        bank_t = [bank(f"bank_t{i}") for i in range(2)]
        bank_g = [bank(f"bank_g{i}") for i in range(FT)]

        const_landed = sem("const_landed")
        pool_const = sem("pool_const")
        dve_const = sem("dve_const")
        act_const = sem("act_const")
        rows_landed = [sem(f"rows_landed{i}") for i in range(2)]
        stat_ready = sem("stat_ready")
        pow_done = sem("pow_done")
        xn_ready = sem("xn_ready")
        xw_scaled = sem("xw_scaled")
        xw_stored = [sem(f"xw_stored{i}") for i in range(2)]
        a_full = sem("a_full")
        a_free = sem("a_free")
        d_full = sem("d_full")
        d_free = sem("d_free")
        t_full = sem("t_full")
        t_free = sem("t_free")
        adj_landed = [sem(f"adj_landed{i}") for i in range(ADJ_SLOTS)]
        adj_free = sem("adj_free")
        g_taken = sem("g_taken")
        x_landed = sem("x_landed")
        x1_ready = sem("x1_ready")
        var_ready = sem("var_ready")
        rstd_ready = sem("rstd_ready")
        xln_ready = sem("xln_ready")
        dve_self = sem("dve_self")
        act_self = sem("act_self")
        hist_saved = sem("hist_saved")
        skip_ready = sem("skip_ready")
        silu_u = sem("silu_u")
        silu_z = sem("silu_z")
        c_ready = sem("c_ready")
        b_stored = sem("b_stored")
        b_landed = [sem(f"b_landed{i}") for i in range(B_SLOTS)]
        soft_ready = sem("soft_ready")
        delta_ready = sem("delta_ready")
        du_ready = sem("du_ready")
        decay_ready = sem("decay_ready")
        drive_ready = sem("drive_ready")
        scanned = sem("scanned")
        saved = sem("saved")
        out_stored = sem("out_stored")

        block = ctx.enter_context(nc.Block())

        CONSTS = [
            (winT, t["winT"].rearrange("(m p) e -> p m e", p=P)),
            (wfc1, t["wfc1"].rearrange("(m p) f -> p m f", p=P)),
            (bfc1, t["bfc1"]),
            (woutM, t["wout"].rearrange("(m p) d -> p m d", p=P)),
            (wfc2T, t["wfc2T"].rearrange("(m p) o -> p m o", p=P)),
            (gnn_w, t["gnn_w"].rearrange("(f p) o -> p f o", p=P)),
            (convw[:], t["conv_w"]), (convb[:], t["conv_b"]), (bdt[:], t["b_dt"]), (dpar[:], t["D"]),
            (amat[:], t["A_log"]),
            (gnn_b[:], t["gnn_b"].partition_broadcast(P)), (fc2_b[:], t["b_fc2"].partition_broadcast(P)),
        ]
        PADDED = [
            (wx[:, :, 0:R + 2 * NS], t["wxT"].rearrange("(i p) e -> p i e", p=P)),
            (wdt[0:R, :], t["wdtT"]),
        ]
        CONST_ALL = 16 * (len(CONSTS) + len(PADDED))

        @block.sync
        def _(sp):
            sp.sem_inc(out_stored, 16)
            for dst, src in CONSTS:
                sp.dma_start(dst, src).then_inc(const_landed, 16)
            sp.wait_ge(pool_const, 2)
            for dst, src in PADDED:
                sp.dma_start(dst, src).then_inc(const_landed, 16)
            with sp.Fori(0, NJ // 2) as jp:
                for b in range(2):
                    sp.wait_ge(xw_scaled, jp * 2 + b + 1)
                    sp.dma_start(rows[:, b, :], t["adj"][bass.ds((jp * 2 + b) * P, P), :]).then_inc(rows_landed[b], 16)
                    sp.dma_start(xj[:, b, :], t["x"][bass.ds((jp * 2 + b) * P, P), :]).then_inc(rows_landed[b], 16)
            for b in range(2):
                sp.wait_ge(xw_stored[b], 16 * (NJ // 2 + 1))
            sp.wait_ge(xw_scaled, NJ + 2)
            with sp.Fori(0, NCH) as k:
                sp.wait_ge(du_ready, (k + 1) * CT)
                sp.dma_start(xin[:], t["x"][bass.ds(k * T, T), :].rearrange("(b p) c -> p b c", p=P)).then_inc(x_landed, 16)
                sp.dma_start(xwi[:], xw_dram[bass.ds(k * T, T), :].rearrange("(b p) c -> p b c", p=P)).then_inc(x_landed, 16)
                for p in range(PAIRS):
                    sp.wait_ge(adj_free, k * PAIRS + p + 1)
                    s = p % ADJ_SLOTS
                    sp.dma_start(adj_r[:, s], t["adjT"][2 * p * P:(2 * p + 2) * P, bass.ds(k * T, T)]
                                 .rearrange("(j p) i -> p j i", p=P)).then_inc(adj_landed[s], 16)
                    sp.dma_start(xw_r[:, s], xw_dram[2 * p * P:(2 * p + 2) * P, :]
                                 .rearrange("(j p) c -> p j c", p=P)).then_inc(adj_landed[s], 16)
                sp.wait_ge(b_stored, (k + 2) * 16)
                for g in range(NG):
                    for s in range(NS):
                        sp.wait_ge(drive_ready, k * UNITS + (g * NS + s + 1 - B_SLOTS) * G + DRIVE_FREE)
                        sp.dma_start(bcast[:, s % B_SLOTS, :],
                                     b_dram[bass.ds(k, 1), s, :].partition_broadcast(P)).then_inc(b_landed[s % B_SLOTS], 16)
                sp.wait_ge(d_free, (k + 1) * D_PER + FREE)
                sp.dma_start(t["out"][bass.ds(k * T, T), :].rearrange("(b p) c -> p b c", p=P), x1[:]).then_inc(out_stored, 16)
            sp.wait_ge(out_stored, 16 * (NCH + 1))

        @block.gpsimd
        def _(pool):
            nc.gpsimd.memset(wx[:], 0.0).then_inc(pool_const, 1)
            nc.gpsimd.memset(wdt[:], 0.0).then_inc(pool_const, 1)
            nc.gpsimd.memset(mhalf[:], -0.5).then_inc(pool_const, 1)
            nc.gpsimd.memset(state[:], 0.0).then_inc(pool_const, 1)
            nc.gpsimd.memset(hist[:], 0.0).then_inc(pool_const, 1)
            nc.gpsimd.memset(ident[:], 0.0).then_inc(pool_const, 1)
            pool.wait_ge(pool_const, 6)
            nc.gpsimd.affine_select(out=ident[:], in_=ident[:], compare_op=ALU.not_equal, fill=1.0, base=0,
                                    pattern=[[-1, P]], channel_multiplier=1).then_inc(pool_const, 1)
            with pool.Fori(0, NJ // 2) as jp:
                for b in range(2):
                    pool.wait_ge(stat_ready, jp * 2 + b + 1)
                    nc.gpsimd.tensor_tensor(srstd[:, b:b + 1], stat[:, b, 1:2], mhalf[:, 0:1], ALU.pow)
                    nc.gpsimd.tensor_tensor(dinv[:, bass.ds(jp * 2 + b, 1)], stat[:, b, 0:1], mhalf[:, 0:1],
                                            ALU.pow).then_inc(pow_done, 1)
            pool.sem_inc(drive_ready, DRIVE_FREE)
            pool.sem_inc(du_ready, CT)
            with pool.Fori(0, NCH) as k:
                pool.wait_ge(var_ready, k + 1)
                nc.gpsimd.tensor_tensor(rstd[:], mv[:, :, 1], mhalf[:], ALU.pow).then_inc(rstd_ready, 1)
                pool.wait_ge(xln_ready, (k + 1) * TB)
                for b in range(TB):
                    nc.gpsimd.tensor_tensor(x1[:, b, :], x1[:, b, :], fc2_b[:], ALU.add).then_inc(x1_ready, 1)
                for i in range(CT):
                    pool.wait_ge(soft_ready, k * CT + i + 1)
                    nc.gpsimd.tensor_tensor(delta[:, i, :], delta[:, i, :], du[:, i, :], ALU.add).then_inc(delta_ready, 1)
                    pool.wait_ge(delta_ready, k * CT + i + 1)
                    nc.gpsimd.tensor_tensor(du[:, i, :], delta[:, i, :], u[:, i, :], ALU.mult).then_inc(du_ready, 1)
                pool.wait_ge(du_ready, (k + 2) * CT)
                for g in range(NG):
                    for s in range(NS):
                        step = g * NS + s
                        b = s % B_SLOTS
                        pool.wait_ge(b_landed[b], (k * (NG * NS // B_SLOTS) + step // B_SLOTS + 1) * 16)
                        for q in range(G):
                            unit = step * G + q
                            pool.wait_ge(scanned, k * UNITS + unit + 1 - DRV_SLOTS + SCAN_FREE)
                            nc.gpsimd.tensor_tensor(drive[:, unit % DRV_SLOTS, :], du[:, g * G + q, :], bcast[:, b, :],
                                                    ALU.mult).then_inc(drive_ready, 1)

        @block.scalar
        def _(act):
            a = Tally(A_PER)

            def take():
                act.wait_ge(a_full, a.next())
                return bank_a[(a.n - 1) % 2]

            def wait_taken():
                act.wait_ge(a_free, a.value() + FREE)

            act.sem_inc(a_free, FREE)
            act.sem_inc(xw_scaled, 2)
            act.sem_inc(saved, NG * NS)
            act.sem_inc(hist_saved, CT)
            act.sem_inc(b_stored, 16)
            for b in range(2):
                act.sem_inc(xw_stored[b], 16)
            act.sem_inc(g_taken, FT)
            act.wait_ge(const_landed, CONST_ALL)
            nc.scalar.activation(amat[:], amat[:], ACT.Exp).then_inc(act_const, 1)
            for f in range(FT):
                for e in range(2 * DI // 512):
                    src = take()
                    nc.scalar.activation(win_c[:, f, e * 512:(e + 1) * 512], src[:], ACT.Copy).then_inc(a_free, 1)
            src = take()
            nc.scalar.activation(bin_c[:], src[:, 0:2 * CT], ACT.Copy).then_inc(a_free, 1)
            for i in range(CT):
                src = take()
                nc.scalar.activation(wout_c[:, i, :], src[:, 0:C], ACT.Copy).then_inc(a_free, 1)
            a.per = 4
            with act.Fori(0, NJ // 2) as jp:
                a.enter(jp)
                for b in range(2):
                    src = take()
                    nc.scalar.activation(xnT[:, b, :], src[:, 0:C], ACT.Copy).then_inc(a_free, 1)
                    src = take()
                    act.wait_ge(pow_done, jp * 2 + b + 1)
                    act.wait_ge(xw_stored[b], (jp + 1) * 16)
                    nc.scalar.activation(xws[:, b, :], src[:, 0:C], ACT.Copy,
                                         scale=dinv[:, bass.ds(jp * 2 + b, 1)]).then_inc(a_free, 1)
                    wait_taken()
                    act.dma_start(xw_dram[bass.ds((jp * 2 + b) * P, P), :], xws[:, b, :]).then_inc(xw_stored[b], 16)
                    act.sem_inc(xw_scaled, 1)
                a.leave(NJ // 2)
            a.per = A_PER
            for b in range(2):
                act.wait_ge(xw_stored[b], 16 * (NJ // 2 + 1))
            act.wait_ge(dve_const, 1 + 4 * CT)
            me = Tally(2 * CT)

            def gnn_out(k):
                act.wait_ge(adj_free, k * PAIRS + PAIRS + ADJ_SLOTS)
                for f in range(FT):
                    nc.scalar.activation(gT[:, f, :], bank_g[f][:], ACT.Copy).then_inc(g_taken, 1)

            def xln_out():
                for f in range(FT):
                    src = take()
                    nc.scalar.activation(xlnT[:, f, :], src[:], ACT.Copy).then_inc(a_free, 1)

            def in_out(k, i):
                src = take()
                act.wait_ge(hist_saved, k * CT + i + 1)
                nc.scalar.activation(upre[:, i % 2, 0:3], hist[:, i, :], ACT.Copy)
                nc.scalar.activation(upre[:, i % 2, 3:T + 3], src[:], ACT.Identity, bias=bin_c[:, i:i + 1]).then_inc(a_free, 1)
                wait_taken()
                nc.scalar.activation(hist[:, i, :], upre[:, i % 2, T:T + 3], ACT.Copy).then_inc(hist_saved, 1)

            def conv_out(i):
                src = take()
                nc.scalar.activation(u[:, i, :], src[:], ACT.Identity, bias=convb[:, i:i + 1]).then_inc(a_free, 1)

            def dbc_out(k):
                src = take()
                act.wait_ge(b_stored, (k + 1) * 16)
                nc.scalar.activation(dbc[:], src[:], ACT.Copy).then_inc(a_free, 1)
                wait_taken()
                act.dma_start(b_dram[bass.ds(k, 1)].rearrange("o s t -> (o s) t"), dbc[R:R + NS, :]).then_inc(b_stored, 16)

            def c_out(k):
                src = take()
                nc.scalar.activation(ccol[:, bass.ds(k * TB, TB), :],
                                     src[:].rearrange("p (b e) -> p b e", b=TB)[:, :, R + NS:R + 2 * NS],
                                     ACT.Copy).then_inc(a_free, 1)
                wait_taken()
                act.sem_inc(c_ready, 1)

            def softplus_terms(i):
                src = take()
                nc.scalar.activation(du[:, i, :], src[:], ACT.Abs, bias=bdt[:, i:i + 1]).then_inc(act_self, 1)
                v = me.next()
                nc.scalar.activation(delta[:, i, :], src[:], ACT.Relu, bias=bdt[:, i:i + 1]).then_inc(a_free, 1)
                act.wait_ge(act_self, v)
                nc.scalar.activation(du[:, i, :], du[:, i, :], ACT.Exp, scale=-1.0).then_inc(act_self, 1)
                act.wait_ge(act_self, me.next())
                nc.scalar.activation(du[:, i, :], du[:, i, :], ACT.Ln, bias=1.0).then_inc(soft_ready, 1)

            def z_out(g):
                for q in range(G):
                    src = take()
                    c = CT + g * G + q
                    nc.scalar.activation(zs[:, q, :], src[:], ACT.Identity, bias=bin_c[:, c:c + 1]).then_inc(a_free, 1)

            def skip_term(k, g):
                n = g * STEPS
                act.wait_ge(t_full, k * T_PER + n * TB)
                for q in range(G):
                    nc.scalar.activation(hbuf[:, n % 2, q, :], u[:, g * G + q, :], ACT.Copy,
                                         scale=dpar[:, g * G + q:g * G + q + 1]).then_inc(skip_ready, 1)

            def decays(k, g, s):
                for q in range(G):
                    unit = (g * NS + s) * G + q
                    act.wait_ge(scanned, k * UNITS + unit + 1 - DEC_SLOTS + SCAN_FREE)
                    nc.scalar.activation(decay[:, unit % DEC_SLOTS, :], delta[:, g * G + q, :], ACT.Exp,
                                         scale=amat[:, g * G + q, s:s + 1]).then_inc(decay_ready, 1)

            def save_state(k, g, s):
                act.wait_ge(scanned, k * UNITS + (g * NS + s + 1) * G + SCAN_FREE)
                nc.scalar.activation(state[:, s, g * G:(g + 1) * G], hbuf[:, (g * STEPS + s + 1) % 2, :, T - 1],
                                     ACT.Copy).then_inc(saved, 1)

            with act.Fori(0, NCH) as k:
                a.enter(k)
                me.enter(k)
                gnn_out(k)
                xln_out()
                act.wait_ge(du_ready, (k + 1) * CT)
                in_out(k, 0)
                for i in range(1, CT):
                    in_out(k, i)
                    conv_out(i - 1)
                conv_out(CT - 1)
                wait_taken()
                for i in range(CT):
                    nc.scalar.activation(u[:, i, :], u[:, i, :], ACT.Silu).then_inc(silu_u, 1)
                dbc_out(k)
                c_out(k)
                act.wait_ge(drive_ready, k * UNITS + DRIVE_FREE)
                for i in range(CT):
                    softplus_terms(i)
                for g in range(NG):
                    act.wait_ge(d_full, k * D_PER + 1 + (2 + g * D_GROUP if g else 0))
                    z_out(g)
                    wait_taken()
                    for q in range(G):
                        nc.scalar.activation(zs[:, q, :], zs[:, q, :], ACT.Silu).then_inc(silu_z, 1)
                    act.wait_ge(silu_u, (k + 1) * CT)
                    skip_term(k, g)
                    act.wait_ge(delta_ready, (k + 1) * CT)
                    for s in range(NS):
                        decays(k, g, s)
                        if s:
                            save_state(k, g, s - 1)
                    save_state(k, g, NS - 1)
                a.leave(NCH)
                me.leave(NCH)

        @block.tensor
        def _(pe):
            a = Tally(A_PER)
            d = Tally(D_PER)

            def fill_a():
                pe.wait_ge(a_free, a.next())
                return bank_a[(a.n - 1) % 2]

            def fill_d():
                pe.wait_ge(d_free, d.next())
                return bank_d[(d.n - 1) % 2]

            def wait_a(use):
                pe.wait_ge(a_free, use + FREE)

            pe.sem_inc(d_full, 1)
            pe.sem_inc(t_full, TB)
            pe.sem_inc(adj_free, ADJ_SLOTS)
            pe.wait_ge(const_landed, CONST_ALL)
            pe.wait_ge(pool_const, 7)
            for f in range(FT):
                for e in range(2 * DI // 512):
                    dst = fill_a()
                    for m in range(KT):
                        mm = nc.tensor.matmul(dst[:], wfc1[:, m, f * P:(f + 1) * P], winT[:, m, e * 512:(e + 1) * 512],
                                              start=(m == 0), stop=(m == KT - 1))
                    mm.then_inc(a_full, 1)
            dst = fill_a()
            for c in range(2 * CT):
                for m in range(KT):
                    mm = nc.tensor.matmul(dst[:, c:c + 1], winT[:, m, c * P:(c + 1) * P], bfc1[:, m:m + 1],
                                          start=(m == 0), stop=(m == KT - 1))
            mm.then_inc(a_full, 1)
            for i in range(CT):
                dst = fill_a()
                for m in range(KT):
                    mm = nc.tensor.matmul(dst[:, 0:C], woutM[:, m, i * P:(i + 1) * P], wfc2T[:, m, :],
                                          start=(m == 0), stop=(m == KT - 1))
                mm.then_inc(a_full, 1)
            a.per = 4
            with pe.Fori(0, NJ // 2) as jp:
                a.enter(jp)
                for b in range(2):
                    pe.wait_ge(xn_ready, jp * 2 + b + 1)
                    dst = fill_a()
                    for f in range(FT):
                        mm = nc.tensor.transpose(dst[:, f * P:(f + 1) * P], xj[:, b, f * P:(f + 1) * P], ident[:])
                    mm.then_inc(a_full, 1)
                    turned = a.value()
                    dst = fill_a()
                    wait_a(turned)
                    for f in range(FT):
                        mm = nc.tensor.matmul(dst[:, 0:C], xnT[:, b, f * P:(f + 1) * P], gnn_w[:, f, :],
                                              start=(f == 0), stop=(f == FT - 1))
                    mm.then_inc(a_full, 1)
                a.leave(NJ // 2)
            a.per = A_PER
            pe.wait_ge(dve_const, 1 + 4 * CT)

            def gnn_product(k, p):
                s = p % ADJ_SLOTS
                pe.wait_ge(adj_landed[s], (k * (PAIRS // ADJ_SLOTS) + p // ADJ_SLOTS + 1) * 32)
                if p == 0:
                    pe.wait_ge(g_taken, (k + 1) * FT)
                for j in range(2):
                    for f in range(FT):
                        mm = nc.tensor.matmul(bank_g[f][:], xw_r[:, s, j, f * P:(f + 1) * P], adj_r[:, s, j, :],
                                              start=(p == 0 and j == 0), stop=(p == PAIRS - 1 and j == 1))
                mm.then_inc(adj_free, 1)

            def gnn_turn(k):
                pe.wait_ge(g_taken, (k + 2) * FT)
                for h in range(TB // 2):
                    dst = fill_d()
                    for b in range(2):
                        for f in range(FT):
                            c = (2 * h + b) * P
                            mm = nc.tensor.transpose(dst[:, b * C + f * P:b * C + (f + 1) * P], gT[:, f, c:c + P], ident[:])
                    mm.then_inc(d_full, 1)

            def xln_turn(k):
                pe.wait_ge(xln_ready, (k + 1) * TB)
                for f in range(FT):
                    dst = fill_a()
                    for b in range(TB):
                        mm = nc.tensor.transpose(dst[:, b * P:(b + 1) * P], xin[:, b, f * P:(f + 1) * P], ident[:])
                    mm.then_inc(a_full, 1)

            def in_product(c):
                dst = fill_a()
                for f in range(FT):
                    mm = nc.tensor.matmul(dst[:], win_c[:, f, c * P:(c + 1) * P], xlnT[:, f, :],
                                          start=(f == 0), stop=(f == FT - 1))
                mm.then_inc(a_full, 1)
                return a.value()

            def conv(i, use):
                dst = fill_a()
                wait_a(use)
                for w in range(4):
                    mm = nc.tensor.matmul(dst[:], diag[:, i, w, :], upre[:, i % 2, w:w + T], start=(w == 0), stop=(w == 3))
                mm.then_inc(a_full, 1)

            def dbc_product(k):
                dst = fill_a()
                for i in range(CT):
                    pe.wait_ge(silu_u, k * CT + i + 1)
                    mm = nc.tensor.matmul(dst[:], wx[:, i, :], u[:, i, :], start=(i == 0), stop=(i == CT - 1))
                mm.then_inc(a_full, 1)
                wait_a(a.value())
                dst = fill_a()
                for b in range(TB):
                    mm = nc.tensor.transpose(dst[:, b * P:(b + 1) * P], dbc[:, b * P:(b + 1) * P], ident[:])
                mm.then_inc(a_full, 1)

            def dt_product(i):
                dst = fill_a()
                nc.tensor.matmul(dst[:], wdt[:, i * P:(i + 1) * P], dbc[:], start=True, stop=True).then_inc(a_full, 1)

            def turn_h(k, g, r):
                n = g * STEPS + r
                if r == 0:
                    pe.wait_ge(skip_ready, k * CT + (g + 1) * G)
                else:
                    pe.wait_ge(scanned, k * UNITS + (g * NS + r) * G + SCAN_FREE)
                for b in range(TB):
                    pe.wait_ge(t_free, k * T_PER + n * TB + b + 1)
                    for q in range(G):
                        mm = nc.tensor.transpose(bank_t[b % 2][:, q * P:(q + 1) * P], hbuf[:, n % 2, q, b * P:(b + 1) * P], ident[:])
                    mm.then_inc(t_full, 1)

            def turn_y(k, g):
                for b in range(TB):
                    pe.wait_ge(t_free, k * T_PER + ((g + 1) * STEPS - 1) * TB + b + 1 + FREE)
                    dst = fill_d()
                    for q in range(G):
                        mm = nc.tensor.transpose(dst[:, q * P:(q + 1) * P], yT[:, b, q * P:(q + 1) * P], ident[:])
                    mm.then_inc(d_full, 1)
                return d.value()

            def out_product(g, last_turn):
                for h in range(TB // 2):
                    dst = fill_d()
                    pe.wait_ge(d_free, last_turn - TB + 2 * h + 2 + FREE)
                    for b in range(2):
                        c = (2 * h + b) * P
                        for q in range(G):
                            mm = nc.tensor.matmul(dst[:, b * C:(b + 1) * C], zs[:, q, c:c + P], wout_c[:, g * G + q, :],
                                                  start=(q == 0), stop=(q == G - 1))
                    mm.then_inc(d_full, 1)

            with pe.Fori(0, NCH) as k:
                a.enter(k)
                d.enter(k)
                for p in range(PAIRS):
                    gnn_product(k, p)
                gnn_turn(k)
                xln_turn(k)
                wait_a(a.value())
                use = in_product(0)
                for i in range(1, CT):
                    ahead = in_product(i)
                    conv(i - 1, use)
                    use = ahead
                conv(CT - 1, use)
                dbc_product(k)
                for i in range(CT):
                    dt_product(i)
                for g in range(NG):
                    for q in range(G):
                        in_product(CT + g * G + q)
                    for r in range(STEPS):
                        turn_h(k, g, r)
                    last = turn_y(k, g)
                    out_product(g, last)
                a.leave(NCH)
                d.leave(NCH)

        @block.vector
        def _(dve):
            d = Tally(D_PER)
            me = Tally(2 * TB + TB // 2 + TB)

            def take():
                dve.wait_ge(d_full, d.next() + 1)
                return bank_d[(d.n - 1) % 2]

            dve.sem_inc(d_free, FREE)
            dve.sem_inc(t_free, FREE)
            dve.sem_inc(scanned, SCAN_FREE)
            dve.wait_ge(act_const, 1)
            nc.vector.tensor_scalar(amat[:], amat[:], -1.0, None, ALU.mult).then_inc(dve_const, 1)
            dve.wait_ge(const_landed, CONST_ALL)
            dve.wait_ge(pool_const, 7)
            for i in range(CT):
                for w in range(4):
                    nc.vector.tensor_scalar(diag[:, i, w, :], ident[:], convw[:, i, w:w + 1], None, ALU.mult).then_inc(dve_const, 1)
            me.per = 2 * 3
            with dve.Fori(0, NJ // 2) as jp:
                me.enter(jp)
                for b in range(2):
                    dve.wait_ge(rows_landed[b], (jp + 1) * 32)
                    nc.vector.reduce_sum(stat[:, b, 0:1], rows[:, b, :], AX_X).then_inc(dve_self, 1)
                    me.next()
                    nc.vector.bn_stats(st[:, b, :], xj[:, b, :]).then_inc(dve_self, 1)
                    dve.wait_ge(dve_self, me.next())
                    nc.vector.tensor_scalar(stat[:, b, 0:1], stat[:, b, 0:1], 1.0, None, ALU.add)
                    nc.vector.bn_aggr(mv[:, b, :], st[:, b, :]).then_inc(dve_self, 1)
                    dve.wait_ge(dve_self, me.next())
                    nc.vector.tensor_scalar(stat[:, b, 1:2], mv[:, b, 1:2], EPS, None, ALU.add).then_inc(stat_ready, 1)
                    dve.wait_ge(pow_done, jp * 2 + b + 1)
                    nc.vector.tensor_scalar(xj[:, b, :], xj[:, b, :], mv[:, b, 0:1], srstd[:, b:b + 1],
                                            ALU.subtract, ALU.mult).then_inc(xn_ready, 1)
                me.leave(NJ // 2)
            me.per = 2 * TB + TB // 2 + TB

            def x1_and_stats(k):
                dve.wait_ge(x_landed, (k + 1) * 32)
                dve.wait_ge(out_stored, (k + 1) * 16)
                for h in range(TB // 2):
                    pair = slice(2 * h, 2 * h + 2)
                    src = take()
                    nc.vector.tensor_tensor(x1[:, pair, :], src[:].rearrange("p (b c) -> p b c", b=2), xwi[:, pair, :],
                                            ALU.add).then_inc(d_free, 1)
                    dve.wait_ge(d_free, d.value() + FREE)
                    for b in range(2 * h, 2 * h + 2):
                        nc.vector.scalar_tensor_tensor(x1[:, b, :], x1[:, b, :], dinv[:, bass.ds(k * TB + b, 1)], gnn_b[:],
                                                       ALU.mult, ALU.add).then_inc(dve_self, 1)
                        v = me.next()
                    dve.wait_ge(dve_self, v)
                    nc.vector.scalar_tensor_tensor(x1[:, pair, :], x1[:, pair, :], 0.0, xin[:, pair, :],
                                                   ALU.max, ALU.add).then_inc(dve_self, 1)
                    dve.wait_ge(dve_self, me.next())
                    for b in range(2 * h, 2 * h + 2):
                        nc.vector.bn_stats(st[:, b, :], x1[:, b, :]).then_inc(dve_self, 1)
                        if b:
                            nc.vector.bn_aggr(mv[:, b - 1, :], st[:, b - 1, :]).then_inc(dve_self, 1)
                            me.next()
                        dve.wait_ge(dve_self, me.next())
                last = TB - 1
                nc.vector.tensor_scalar(mv[:, 0:last, 1], mv[:, 0:last, 1], EPS, None, ALU.add)
                nc.vector.bn_aggr(mv[:, last, :], st[:, last, :]).then_inc(dve_self, 1)
                dve.wait_ge(dve_self, me.next())
                nc.vector.tensor_scalar(mv[:, last, 1:2], mv[:, last, 1:2], EPS, None, ALU.add).then_inc(var_ready, 1)

            def xln(k):
                dve.wait_ge(rstd_ready, k + 1)
                for b in range(TB):
                    nc.vector.tensor_scalar(xin[:, b, :], x1[:, b, :], mv[:, b, 0:1], rstd[:, b:b + 1],
                                            ALU.subtract, ALU.mult).then_inc(xln_ready, 1)

            def scan(k, g, s, q):
                unit = (g * NS + s) * G + q
                n = g * STEPS + s + 1
                if q == 0:
                    dve.wait_ge(t_full, k * T_PER + n * TB)
                    dve.wait_ge(saved, (k + 1) * (NG * NS) + g * NS + max(s - 1, 0))
                dve.wait_ge(decay_ready, k * UNITS + unit + 1)
                dve.wait_ge(drive_ready, k * UNITS + unit + 1 + DRIVE_FREE)
                nc.vector.tensor_tensor_scan(hbuf[:, n % 2, q, :], decay[:, unit % DEC_SLOTS, :], drive[:, unit % DRV_SLOTS, :],
                                             state[:, s, g * G + q:g * G + q + 1], ALU.mult, ALU.add).then_inc(scanned, 1)

            def add_up(k, g, r, b):
                use = k * T_PER + (g * STEPS + r) * TB + b
                dve.wait_ge(t_full, use + 1 + TB)
                if r == 0:
                    dve.wait_ge(d_full, k * D_PER + 1 + (2 + D_GROUP * g - TB // 2 if g else 0))
                    nc.vector.tensor_copy(yT[:, b, :], bank_t[b % 2][:]).then_inc(t_free, 1)
                else:
                    dve.wait_ge(t_free, use - TB + 1 + FREE)
                    nc.vector.scalar_tensor_tensor(yT[:, b, :], bank_t[b % 2][:], ccol[:, bass.ds(k * TB + b, 1), r - 1],
                                                   yT[:, b, :], ALU.mult, ALU.add).then_inc(t_free, 1)

            def gate(k, g):
                dve.wait_ge(silu_z, k * CT + (g + 1) * G)
                for b in range(TB):
                    src = take()
                    block_ = zs[:, :, b * P:(b + 1) * P]
                    nc.vector.tensor_tensor(block_, src[:].rearrange("p (q t) -> p q t", q=G), block_, ALU.mult).then_inc(d_free, 1)

            def add_out(k):
                dve.wait_ge(x1_ready, (k + 1) * TB)
                for h in range(TB // 2):
                    src = take()
                    pair = slice(2 * h, 2 * h + 2)
                    nc.vector.tensor_tensor(x1[:, pair, :], src[:].rearrange("p (b c) -> p b c", b=2), x1[:, pair, :],
                                            ALU.add).then_inc(d_free, 1)

            with dve.Fori(0, NCH) as k:
                d.enter(k)
                me.enter(k)
                x1_and_stats(k)
                xln(k)
                dve.wait_ge(c_ready, k + 1)
                for g in range(NG):
                    for b in range(TB):
                        add_up(k, g, 0, b)
                    for s in range(NS):
                        for q in range(G):
                            scan(k, g, s, q)
                            if s:
                                add_up(k, g, s, q)
                    for b in range(TB):
                        add_up(k, g, NS, b)
                    gate(k, g)
                    add_out(k)
                d.leave(NCH)
                me.leave(NCH)


INPUTS = ("adj", "adjT", "x", "gnn_w", "gnn_b", "wfc1", "bfc1", "winT", "conv_w", "conv_b", "wxT", "wdtT", "b_dt",
          "A_log", "D", "wout", "wfc2T", "b_fc2")


def kernel(x, adj, L0_gnn_W, L0_gnn_b, L0_ffn_W_fc1, L0_ffn_b_fc1, L0_ffn_W_in, L0_ffn_conv_w, L0_ffn_conv_b,
           L0_ffn_W_xproj, L0_ffn_W_dt, L0_ffn_b_dt, L0_ffn_A_log, L0_ffn_D, L0_ffn_W_out, L0_ffn_W_fc2, L0_ffn_b_fc2):
    import concourse.bacc as bacc
    from concourse.bass_utils import run_bass_kernel_spmd

    def by_channel(v):
        v = np.asarray(v)
        w = v.reshape(v.shape[0] // P, P, -1).transpose(1, 0, 2)
        return w if v.ndim > 1 else w[:, :, 0]

    arrays = dict(
        adj=adj, adjT=np.asarray(adj).T, x=x, gnn_w=np.asarray(L0_gnn_W).T, gnn_b=L0_gnn_b, wfc1=L0_ffn_W_fc1,
        bfc1=by_channel(L0_ffn_b_fc1), winT=np.asarray(L0_ffn_W_in).T, conv_w=by_channel(L0_ffn_conv_w),
        conv_b=by_channel(L0_ffn_conv_b), wxT=np.asarray(L0_ffn_W_xproj).T, wdtT=np.asarray(L0_ffn_W_dt).T,
        b_dt=by_channel(L0_ffn_b_dt), A_log=by_channel(L0_ffn_A_log), D=by_channel(L0_ffn_D), wout=L0_ffn_W_out,
        wfc2T=np.asarray(L0_ffn_W_fc2).T, b_fc2=L0_ffn_b_fc2)
    arrays = {"in_" + n: np.ascontiguousarray(arrays[n]) for n in INPUTS}
    nc = bacc.Bacc("TRN2", target_bir_lowering=False, num_devices=1)
    t = {n: nc.dram_tensor("in_" + n, arrays["in_" + n].shape, F32, kind="ExternalInput").ap() for n in INPUTS}
    t["out"] = nc.dram_tensor("out", [N, C], F32, kind="ExternalOutput").ap()
    build(nc, t)
    return run_bass_kernel_spmd(nc, [arrays], core_ids=[0]).results[0]["out"]
```

```python
from contextlib import ExitStack

import numpy as np

import concourse.bass as bass
from concourse import mybir

F32 = mybir.dt.float32
ACT = mybir.ActivationFunctionType
ALU = mybir.AluOpType
AX_X = mybir.AxisListType.X

P = 128
N = 4096
C = 256
DM = 512
DI = 1024
NS = 16
R = 32
T = 512
NCH = N // T
TB = T // P
CT = DI // P
G = 4
NG = CT // G
FT = C // P
KT = DM // P
NJ = N // P
STEPS = NS + 1
EPS = 1e-5
ADJ_SLOTS = 4
DEC_SLOTS = 4
DRV_SLOTS = 4
B_SLOTS = 4
FREE = 2


class Tally:

    def __init__(self, per=0):
        self.per, self.n, self.base = per, 0, 0

    def next(self):
        self.n += 1
        return self.base + self.n

    def value(self):
        return self.base + self.n

    def enter(self, k):
        self.start, self.base = self.n, k * self.per

    def leave(self, times):
        assert self.n - self.start == self.per, (self.n - self.start, self.per)
        self.n, self.base = self.start + times * self.per, 0


UNITS = NG * NS * G
SCAN_FREE = DEC_SLOTS
DRIVE_FREE = B_SLOTS * G

ACT_LAG = 9
GNN_AT = [4 + (j * 52) // (2 * NJ) for j in range(2 * NJ)]
OUT_AT = [12, 13, 14, 15]
DT_HIGH_AT = [18, 22, 26, 30]
Z_LOW_AT = [56, 59, 60, 61]
GT_AT = [57, 58]
XLN_AT = [66, 67]
IN_AT = [70 + 5 * i for i in range(CT)]
CONV_AT = [73 + 5 * i for i in range(CT)]
OUT_LOW_AT = [80, 81, 85, 86]
Z_HIGH_AT = [90, 91, 95, 96]
DBC_AT = [111, 112, 113, 114]
C_AT = 117
DT_LOW_AT = [118, 119, 120, 121]
SILU_LOW_AT = CONV_AT[3] + 1 + ACT_LAG
SILU_HIGH_AT = CONV_AT[7] + 1 + ACT_LAG
ADJ_BY = [0] + [min(NJ, (j + 1) * NJ // 13 + 2) for j in range(NG * NS)]

A_PER = 2 + CT + CT + 1 + 1 + CT + CT
D_GROUP = TB + TB // 2
D_PER = 2 + NG * D_GROUP
T_PER = NG * STEPS * TB


def build(nc, t):
    nc.disable_value_cache = True
    ctx = ExitStack()
    with ctx:
        def sb(name, *shape):
            return ctx.enter_context(nc.sbuf_tensor(name, [P, *shape], F32))

        def sem(name):
            return ctx.enter_context(nc.semaphore(name))

        xw_dram = nc.dram_tensor("xw_scratch", [N, C], F32, kind="Internal").ap()
        b_dram = nc.dram_tensor("b_scratch", [NCH, NS, T], F32, kind="Internal").ap()

        win_c = sb("win_c", FT, 2 * DI)
        wout_c = sb("wout_c", CT, C)
        wx = sb("wx", CT, P)
        wdt = sb("wdt", DI)
        diag = sb("diag", CT, 4, P)
        ident = sb("ident", P)
        bin_c = sb("bin_c", 2 * CT)
        convw = sb("convw", CT, 4)
        convb = sb("convb", CT)
        bdt = sb("bdt", CT)
        dpar = sb("dpar", CT)
        amat = sb("amat", CT, NS)
        gnn_b = sb("gnn_b", C)
        fc2_b = sb("fc2_b", C)
        mhalf = sb("mhalf", TB)
        dinv = sb("dinv", NJ)
        adj_r = sb("adj_r", ADJ_SLOTS, T)
        xw_r = sb("xw_r", ADJ_SLOTS, C)
        xin = sb("xin", TB, C)
        xwi = sb("xwi", TB, C)
        x1 = sb("x1", TB, C)
        mv = sb("mv", TB, 2)
        st = sb("st", TB, 6)
        rstd = sb("rstd", TB)
        xlnT = sb("xlnT", 2 * FT, T)
        xo = sb("xo", TB, C)
        upre = sb("upre", 2, T + 3)
        hist = sb("hist", CT, 3)
        dbc = sb("dbc", T)
        ccol = sb("ccol", NCH * TB, NS)
        bcast = sb("bcast", B_SLOTS, T)
        state = sb("state", NS, CT)
        yT = sb("yT", TB, G * P)
        big = sb("big", 14336)
        u = big[:, 0:4096].rearrange("p (i t) -> p i t", t=T)
        hbuf = big[:, 4096:8192].rearrange("p (b q t) -> p b q t", b=2, t=T)
        decay = big[:, 8192:10240].rearrange("p (b t) -> p b t", t=T)
        du = big[:, 10240:14336].rearrange("p (i t) -> p i t", t=T)
        big2 = sb("big2", 8192)
        delta = big2[:, 0:4096].rearrange("p (i t) -> p i t", t=T)
        zs = big2[:, 4096:6144].rearrange("p (q t) -> p q t", t=T)
        drive = big2[:, 6144:8192].rearrange("p (b t) -> p b t", t=T)
        winT = big[:, 0:8192].rearrange("p (m e) -> p m e", m=KT)
        woutM = big[:, 8192:12288].rearrange("p (m d) -> p m d", m=KT)
        wfc1 = big[:, 12288:13312].rearrange("p (m f) -> p m f", m=KT)
        wfc2T = big[:, 13312:14336].rearrange("p (m o) -> p m o", m=KT)
        gnn_w = yT[:, 0, :].rearrange("p (f o) -> p f o", f=FT)
        bfc1 = yT[:, 1, 0:KT]
        rows = big2[:, :].rearrange("p (b n) -> p b n", b=2)
        xj = xin[:, 0:2, :]
        xws = x1[:, 0:2, :]
        xnT = xwi[:, 0:2, :]
        stat = sb("stat", 2, 2)
        srstd = sb("srstd", 2)
        gT = upre[:, :, 0:T]

        def bank(name):
            return ctx.enter_context(nc.psum_tensor(name, [P, 512], F32))
        bank_a = [bank(f"bank_a{i}") for i in range(2)]
        bank_d = [bank(f"bank_d{i}") for i in range(2)]
        bank_t = [bank(f"bank_t{i}") for i in range(2)]
        bank_g = [bank(f"bank_g{i}") for i in range(FT)]

        const_landed = sem("const_landed")
        pool_const = sem("pool_const")
        dve_const = sem("dve_const")
        act_const = sem("act_const")
        rows_landed = [sem(f"rows_landed{i}") for i in range(2)]
        stat_ready = sem("stat_ready")
        pow_done = sem("pow_done")
        xn_ready = sem("xn_ready")
        xj_landed = [sem(f"xj_landed{i}") for i in range(2)]
        adj0_landed = [sem(f"adj0_landed{i}") for i in range(2)]
        rows_free = sem("rows_free")
        xw_stored = [sem(f"xw_stored{i}") for i in range(2)]
        a_full = sem("a_full")
        a_free = sem("a_free")
        d_full = sem("d_full")
        d_free = sem("d_free")
        t_full = sem("t_full")
        t_free = sem("t_free")
        adj_landed = [sem(f"adj_landed{i}") for i in range(ADJ_SLOTS)]
        adj_free = sem("adj_free")
        g_taken = sem("g_taken")
        x_landed = sem("x_landed")
        xo_ready = sem("xo_ready")
        var_ready = sem("var_ready")
        rstd_ready = sem("rstd_ready")
        xln_ready = sem("xln_ready")
        dve_self = sem("dve_self")
        act_self = sem("act_self")
        hist_saved = sem("hist_saved")
        skip_ready = sem("skip_ready")
        silu_u = sem("silu_u")
        silu_z = sem("silu_z")
        c_ready = sem("c_ready")
        b_stored = sem("b_stored")
        b_landed = [sem(f"b_landed{i}") for i in range(B_SLOTS)]
        soft_ready = sem("soft_ready")
        delta_ready = sem("delta_ready")
        du_ready = sem("du_ready")
        decay_ready = sem("decay_ready")
        drive_ready = sem("drive_ready")
        scanned = sem("scanned")
        saved = sem("saved")
        out_stored = sem("out_stored")

        block = ctx.enter_context(nc.Block())

        CONSTS = [
            (winT, t["winT"].rearrange("(m p) e -> p m e", p=P)),
            (wfc1, t["wfc1"].rearrange("(m p) f -> p m f", p=P)),
            (bfc1, t["bfc1"]),
            (woutM, t["wout"].rearrange("(m p) d -> p m d", p=P)),
            (wfc2T, t["wfc2T"].rearrange("(m p) o -> p m o", p=P)),
            (gnn_w, t["gnn_w"].rearrange("(f p) o -> p f o", p=P)),
            (convw[:], t["conv_w"]), (convb[:], t["conv_b"]), (bdt[:], t["b_dt"]), (dpar[:], t["D"]),
            (amat[:], t["A_log"]),
            (gnn_b[:], t["gnn_b"].partition_broadcast(P)), (fc2_b[:], t["b_fc2"].partition_broadcast(P)),
        ]
        PADDED = [
            (wx[:, :, 0:R + 2 * NS], t["wxT"].rearrange("(i p) e -> p i e", p=P)),
            (wdt[0:R, :], t["wdtT"]),
        ]
        CONST_ALL = 16 * (len(CONSTS) + len(PADDED))

        @block.sync
        def _(sp):
            sp.sem_inc(out_stored, 16)
            for dst, src in CONSTS:
                sp.dma_start(dst, src).then_inc(const_landed, 16)
            sp.wait_ge(pool_const, 2)
            for dst, src in PADDED:
                sp.dma_start(dst, src).then_inc(const_landed, 16)
            with sp.Fori(0, NJ // 2) as jp:
                for b in range(2):
                    sp.wait_ge(rows_free, jp * 2 + b + 1)
                    sp.dma_start(rows[:, b, :], t["adj"][bass.ds((jp * 2 + b) * P, P), :]).then_inc(rows_landed[b], 16)
                    sp.wait_ge(adj_free, jp * 2 + b + 2)
                    sp.dma_start(xj[:, b, :], t["x"][bass.ds((jp * 2 + b) * P, P), :]).then_inc(xj_landed[b], 16)
                    sp.dma_start(adj_r[:, b, :], t["adjT"][bass.ds((jp * 2 + b) * P, P), 0:T]).then_inc(adj0_landed[b], 16)
            for b in range(2):
                sp.wait_ge(xw_stored[b], 16 * (NJ // 2 + 1))
            sp.wait_ge(adj_free, NJ + ADJ_SLOTS)

            def load_own(c):
                sp.dma_start(xin[:], t["x"][bass.ds(c * T, T), :].rearrange("(b p) c -> p b c", p=P)).then_inc(x_landed, 16)
                sp.dma_start(xwi[:], xw_dram[bass.ds(c * T, T), :].rearrange("(b p) c -> p b c", p=P)).then_inc(x_landed, 16)

            def load_adj(c, j):
                s = j % ADJ_SLOTS
                sp.wait_ge(adj_free, c * NJ + j + 1)
                sp.dma_start(adj_r[:, s, :], t["adjT"][j * P:(j + 1) * P, bass.ds(c * T, T)]).then_inc(adj_landed[s], 16)
                sp.dma_start(xw_r[:, s, :], xw_dram[j * P:(j + 1) * P, :]).then_inc(adj_landed[s], 16)

            def load_b(c, step):
                sp.wait_ge(drive_ready, c * UNITS + (step + 1 - B_SLOTS) * G + DRIVE_FREE)
                sp.dma_start(bcast[:, step % B_SLOTS, :],
                             b_dram[bass.ds(c, 1), step % NS, :].partition_broadcast(P)).then_inc(b_landed[step % B_SLOTS], 16)

            def store_out(c, last=False):
                sp.wait_ge(d_free, (c + 1) * D_PER + (0 if last else 2) + FREE)
                sp.dma_start(t["out"][bass.ds(c * T, T), :].rearrange("(b p) c -> p b c", p=P), xo[:]).then_inc(out_stored, 16)

            def chunk(k, first=False, last=False):
                if not last:
                    sp.wait_ge(silu_u, (k + 1) * CT)
                    load_own(k + 1)
                for j in range(NG * NS):
                    if not last:
                        for i in range(ADJ_BY[j], ADJ_BY[j + 1]):
                            load_adj(k + 1, i)
                        if j == NG * NS - B_SLOTS:
                            sp.wait_ge(b_stored, (k + 3) * 16)
                    if j + B_SLOTS < NG * NS:
                        load_b(k, j + B_SLOTS)
                    elif not last:
                        load_b(k + 1, j + B_SLOTS - NG * NS)
                    if j == 6 and not first:
                        store_out(k - 1)

            load_own(0)
            sp.wait_ge(b_stored, 2 * 16)
            for step in range(B_SLOTS):
                load_b(0, step)
            chunk(0, first=True)
            with sp.Fori(1, NCH - 1) as k:
                chunk(k)
            chunk(NCH - 1, last=True)
            store_out(NCH - 1, last=True)
            sp.wait_ge(out_stored, 16 * (NCH + 1))

        @block.gpsimd
        def _(pool):
            nc.gpsimd.memset(wx[:], 0.0).then_inc(pool_const, 1)
            nc.gpsimd.memset(wdt[:], 0.0).then_inc(pool_const, 1)
            nc.gpsimd.memset(mhalf[:], -0.5).then_inc(pool_const, 1)
            nc.gpsimd.memset(state[:], 0.0).then_inc(pool_const, 1)
            nc.gpsimd.memset(hist[:], 0.0).then_inc(pool_const, 1)
            nc.gpsimd.memset(ident[:], 0.0).then_inc(pool_const, 1)
            pool.wait_ge(pool_const, 6)
            nc.gpsimd.affine_select(out=ident[:], in_=ident[:], compare_op=ALU.not_equal, fill=1.0, base=0,
                                    pattern=[[-1, P]], channel_multiplier=1).then_inc(pool_const, 1)
            with pool.Fori(0, NJ // 2) as jp:
                for b in range(2):
                    pool.wait_ge(stat_ready, jp * 2 + b + 1)
                    nc.gpsimd.tensor_tensor(srstd[:, b:b + 1], stat[:, b, 1:2], mhalf[:, 0:1], ALU.pow)
                    nc.gpsimd.tensor_tensor(dinv[:, bass.ds(jp * 2 + b, 1)], stat[:, b, 0:1], mhalf[:, 0:1],
                                            ALU.pow).then_inc(pow_done, 1)
            pool.sem_inc(drive_ready, DRIVE_FREE)
            pool.sem_inc(du_ready, CT)

            def rstd_of(c):
                pool.wait_ge(var_ready, c + 1)
                nc.gpsimd.tensor_tensor(rstd[:], mv[:, :, 1], mhalf[:], ALU.pow).then_inc(rstd_ready, 1)

            def start_out(k):
                pool.wait_ge(out_stored, (k + 1) * 16)
                pool.wait_ge(xln_ready, (k + 1) * TB)
                for b in range(TB):
                    nc.gpsimd.tensor_tensor(xo[:, b, :], x1[:, b, :], fc2_b[:], ALU.add).then_inc(xo_ready, 1)

            def delta_du(c, i):
                pool.wait_ge(soft_ready, c * CT + i + 1)
                nc.gpsimd.tensor_tensor(delta[:, i, :], delta[:, i, :], du[:, i, :], ALU.add).then_inc(delta_ready, 1)
                pool.wait_ge(delta_ready, c * CT + i + 1)
                nc.gpsimd.tensor_tensor(du[:, i, :], delta[:, i, :], u[:, i, :], ALU.mult).then_inc(du_ready, 1)

            def drive_of(k, g, s, q):
                unit = (g * NS + s) * G + q
                if q == 0:
                    pool.wait_ge(b_landed[s % B_SLOTS], (k * (NG * NS // B_SLOTS) + (g * NS + s) // B_SLOTS + 1) * 16)
                    if s == 0:
                        pool.wait_ge(du_ready, (k + 1) * CT + (g + 1) * G)
                pool.wait_ge(scanned, k * UNITS + unit + 1 - DRV_SLOTS + SCAN_FREE)
                nc.gpsimd.tensor_tensor(drive[:, unit % DRV_SLOTS, :], du[:, g * G + q, :], bcast[:, s % B_SLOTS, :],
                                        ALU.mult).then_inc(drive_ready, 1)

            def chunk(k, last=False):
                for g in range(NG):
                    for s in range(NS):
                        for q in range(G):
                            x = (g * STEPS + s + 1) * TB + q
                            if x == STEPS * TB + TB and not last:
                                rstd_of(k + 1)
                            drive_of(k, g, s, q)
                            if x - 1 - ACT_LAG in DT_HIGH_AT:
                                delta_du(k, G + DT_HIGH_AT.index(x - 1 - ACT_LAG))
                            if x - 1 - ACT_LAG in DT_LOW_AT and not last:
                                delta_du(k + 1, DT_LOW_AT.index(x - 1 - ACT_LAG))
                            if x == 9 * TB:
                                start_out(k)

            rstd_of(0)
            for i in range(G):
                delta_du(0, i)
            chunk(0)
            with pool.Fori(1, NCH - 1) as k:
                chunk(k)
            chunk(NCH - 1, last=True)

        @block.scalar
        def _(act):
            a = Tally(A_PER)

            def take():
                act.wait_ge(a_full, a.next())
                return bank_a[(a.n - 1) % 2]

            def wait_taken():
                act.wait_ge(a_free, a.value() + FREE)

            act.sem_inc(a_free, FREE)
            act.sem_inc(saved, NG * NS)
            act.sem_inc(hist_saved, CT)
            act.sem_inc(b_stored, 16)
            for b in range(2):
                act.sem_inc(xw_stored[b], 16)
            act.sem_inc(g_taken, FT)
            act.wait_ge(const_landed, CONST_ALL)
            nc.scalar.activation(amat[:], amat[:], ACT.Exp).then_inc(act_const, 1)
            src = take()
            nc.scalar.activation(bin_c[:], src[:, 0:2 * CT], ACT.Copy).then_inc(a_free, 1)
            for i in range(CT):
                src = take()
                nc.scalar.activation(wout_c[:, i, :], src[:, 0:C], ACT.Copy).then_inc(a_free, 1)
            a.per = 6
            with act.Fori(0, NJ // 2) as jp:
                a.enter(jp)
                for b in range(2):
                    src = take()
                    nc.scalar.activation(win_c[:, b, bass.ds(jp * P, P)], src[:, 0:P], ACT.Copy).then_inc(a_free, 1)
                    src = take()
                    nc.scalar.activation(xnT[:, b, :], src[:, 0:C], ACT.Copy).then_inc(a_free, 1)
                    src = take()
                    act.wait_ge(pow_done, jp * 2 + b + 1)
                    act.wait_ge(xw_stored[b], (jp + 1) * 16)
                    act.wait_ge(adj_free, jp * 2 + b + 2)
                    nc.scalar.activation(xws[:, b, :], src[:, 0:C], ACT.Copy,
                                         scale=dinv[:, bass.ds(jp * 2 + b, 1)]).then_inc(a_free, 1)
                    wait_taken()
                    act.dma_start(xw_dram[bass.ds((jp * 2 + b) * P, P), :], xws[:, b, :]).then_inc(xw_stored[b], 16)
                a.leave(NJ // 2)
            a.per = A_PER
            for b in range(2):
                act.wait_ge(xw_stored[b], 16 * (NJ // 2 + 1))
            act.wait_ge(dve_const, 1 + 4 * CT)
            me = Tally(2 * CT)

            def gnn_out(k):
                act.wait_ge(adj_free, (k + 1) * NJ + ADJ_SLOTS)
                for f in range(FT):
                    nc.scalar.activation(gT[:, f, :], bank_g[f][:], ACT.Copy).then_inc(g_taken, 1)

            def xln_out(k, f):
                src = take()
                nc.scalar.activation(xlnT[:, bass.ds((k % 2) * FT + f, 1), :].rearrange("p o t -> p (o t)"), src[:],
                                     ACT.Copy).then_inc(a_free, 1)

            def in_out(k, i):
                src = take()
                act.wait_ge(hist_saved, k * CT + i + 1)
                nc.scalar.activation(upre[:, i % 2, 0:3], hist[:, i, :], ACT.Copy)
                nc.scalar.activation(upre[:, i % 2, 3:T + 3], src[:], ACT.Identity, bias=bin_c[:, i:i + 1]).then_inc(a_free, 1)
                wait_taken()
                nc.scalar.activation(hist[:, i, :], upre[:, i % 2, T:T + 3], ACT.Copy).then_inc(hist_saved, 1)

            def conv_out(i):
                src = take()
                nc.scalar.activation(u[:, i, :], src[:], ACT.Identity, bias=convb[:, i:i + 1]).then_inc(a_free, 1)

            def dbc_out(k):
                src = take()
                act.wait_ge(b_stored, (k + 1) * 16)
                nc.scalar.activation(dbc[:], src[:], ACT.Copy).then_inc(a_free, 1)
                wait_taken()
                act.dma_start(b_dram[bass.ds(k, 1)].rearrange("o s t -> (o s) t"), dbc[R:R + NS, :]).then_inc(b_stored, 16)

            def c_out(k):
                src = take()
                nc.scalar.activation(ccol[:, bass.ds(k * TB, TB), :],
                                     src[:].rearrange("p (b e) -> p b e", b=TB)[:, :, R + NS:R + 2 * NS],
                                     ACT.Copy).then_inc(a_free, 1)
                wait_taken()
                act.sem_inc(c_ready, 1)

            def softplus_terms(i):
                src = take()
                nc.scalar.activation(du[:, i, :], src[:], ACT.Abs, bias=bdt[:, i:i + 1]).then_inc(act_self, 1)
                v = me.next()
                nc.scalar.activation(delta[:, i, :], src[:], ACT.Relu, bias=bdt[:, i:i + 1]).then_inc(a_free, 1)
                act.wait_ge(act_self, v)
                nc.scalar.activation(du[:, i, :], du[:, i, :], ACT.Exp, scale=-1.0).then_inc(act_self, 1)
                act.wait_ge(act_self, me.next())
                nc.scalar.activation(du[:, i, :], du[:, i, :], ACT.Ln, bias=1.0).then_inc(soft_ready, 1)

            def z_out(c):
                src = take()
                nc.scalar.activation(zs[:, c % G, :], src[:], ACT.Identity, bias=bin_c[:, CT + c:CT + c + 1]).then_inc(a_free, 1)

            def exp_tables():
                nc.scalar.preload_act_table_set("natural_log_exp_and_others")

            def silu_of_z():
                for q in range(G):
                    nc.scalar.activation(zs[:, q, :], zs[:, q, :], ACT.Silu).then_inc(silu_z, 1)

            def silu_of_u(half):
                for i in range(half * G, (half + 1) * G):
                    nc.scalar.activation(u[:, i, :], u[:, i, :], ACT.Silu).then_inc(silu_u, 1)

            def skip_term(k, g):
                n = g * STEPS
                act.wait_ge(t_full, k * T_PER + n * TB)
                act.wait_ge(saved, (k + 1) * (NG * NS) + g * NS - 1)
                for q in range(G):
                    nc.scalar.activation(hbuf[:, n % 2, q, :], u[:, g * G + q, :], ACT.Copy,
                                         scale=dpar[:, g * G + q:g * G + q + 1]).then_inc(skip_ready, 1)

            def decay_of(k, g, s, q):
                unit = (g * NS + s) * G + q
                act.wait_ge(scanned, k * UNITS + unit + 1 - DEC_SLOTS + SCAN_FREE)
                nc.scalar.activation(decay[:, unit % DEC_SLOTS, :], delta[:, g * G + q, :], ACT.Exp,
                                     scale=amat[:, g * G + q, s:s + 1]).then_inc(decay_ready, 1)

            def save_state(k, g, s):
                act.wait_ge(scanned, k * UNITS + (g * NS + s + 1) * G + SCAN_FREE)
                nc.scalar.activation(state[:, s, g * G:(g + 1) * G], hbuf[:, (g * STEPS + s + 1) % 2, :, T - 1],
                                     ACT.Copy).then_inc(saved, 1)

            def beside(k, x, first, last):
                y = x - ACT_LAG
                if y in DT_HIGH_AT:
                    if y == DT_HIGH_AT[0]:
                        act.wait_ge(drive_ready, k * UNITS + DRIVE_FREE)
                    softplus_terms(G + DT_HIGH_AT.index(y))
                if y in Z_LOW_AT:
                    if y == Z_LOW_AT[0] and not first:
                        act.wait_ge(d_full, k * D_PER + 2 + 1)
                    z_out(Z_LOW_AT.index(y))
                    if y == Z_LOW_AT[-1]:
                        wait_taken()
                        silu_of_z()
                        exp_tables()
                if y in Z_HIGH_AT:
                    if y == Z_HIGH_AT[0]:
                        act.wait_ge(d_full, k * D_PER + (8 if last else 10) + 1)
                    z_out(G + Z_HIGH_AT.index(y))
                if x == SILU_HIGH_AT and last:
                    wait_taken()
                    silu_of_z()
                    exp_tables()
                if last:
                    return
                if y == GNN_AT[-1]:
                    gnn_out(k + 1)
                if y in XLN_AT:
                    xln_out(k + 1, XLN_AT.index(y))
                if y in IN_AT:
                    in_out(k + 1, IN_AT.index(y))
                if y - 1 in CONV_AT:
                    if y - 1 == CONV_AT[0]:
                        act.wait_ge(du_ready, (k + 2) * CT)
                    conv_out(CONV_AT.index(y - 1))
                if x == SILU_LOW_AT:
                    wait_taken()
                    silu_of_u(0)
                    exp_tables()
                if x == SILU_HIGH_AT:
                    wait_taken()
                    silu_of_u(1)
                    silu_of_z()
                    exp_tables()
                if y == DBC_AT[-1]:
                    dbc_out(k + 1)
                if y == C_AT:
                    c_out(k + 1)
                if y in DT_LOW_AT:
                    if y == DT_LOW_AT[0]:
                        act.wait_ge(drive_ready, k * UNITS + NS * G + DRIVE_FREE)
                    softplus_terms(DT_LOW_AT.index(y))

            def chunk(k, first=False, last=False):
                for g in range(NG):
                    for r in range(STEPS):
                        for q in range(G):
                            x = (g * STEPS + r) * TB + q
                            if r:
                                if r == 1 and q == 0:
                                    act.wait_ge(delta_ready, k * CT + (g + 1) * G)
                                decay_of(k, g, r - 1, q)
                            beside(k, x, first, last)
                        if r == 1:
                            if g:
                                save_state(k, 0, NS - 1)
                            elif not first:
                                save_state(k - 1, NG - 1, NS - 1)
                            act.wait_ge(silu_u, (k + 1) * CT)
                            skip_term(k, g)
                        if r > 1:
                            save_state(k, g, r - 2)

            gnn_out(0)
            for f in range(FT):
                xln_out(0, f)
            for i in range(CT):
                in_out(0, i)
                conv_out(i)
            wait_taken()
            for half in range(2):
                silu_of_u(half)
            exp_tables()
            dbc_out(0)
            c_out(0)
            for i in range(G):
                softplus_terms(i)
            chunk(0, first=True)
            with act.Fori(1, NCH - 1) as k:
                a.enter(k - 1)
                me.enter(k - 1)
                chunk(k)
                a.leave(NCH - 2)
                me.leave(NCH - 2)
            chunk(NCH - 1, last=True)

        @block.tensor
        def _(pe):
            a = Tally(A_PER)
            d = Tally(D_PER)

            def fill_a():
                pe.wait_ge(a_free, a.next())
                return bank_a[(a.n - 1) % 2]

            def fill_d():
                pe.wait_ge(d_free, d.next())
                return bank_d[(d.n - 1) % 2]

            def wait_a(use):
                pe.wait_ge(a_free, use + FREE)

            pe.sem_inc(d_full, 1)
            pe.sem_inc(t_full, TB)
            pe.sem_inc(adj_free, ADJ_SLOTS - 1)
            pe.wait_ge(const_landed, CONST_ALL)
            pe.wait_ge(pool_const, 7)
            dst = fill_a()
            for c in range(2 * CT):
                for m in range(KT):
                    mm = nc.tensor.matmul(dst[:, c:c + 1], winT[:, m, c * P:(c + 1) * P], bfc1[:, m:m + 1],
                                          start=(m == 0), stop=(m == KT - 1))
            mm.then_inc(a_full, 1)
            for i in range(CT):
                dst = fill_a()
                for m in range(KT):
                    mm = nc.tensor.matmul(dst[:, 0:C], woutM[:, m, i * P:(i + 1) * P], wfc2T[:, m, :],
                                          start=(m == 0), stop=(m == KT - 1))
                mm.then_inc(a_full, 1)
            for f in range(FT):
                nc.tensor.matmul(bank_g[f][:], state[:].rearrange("p s i -> p (s i)"), winT[:, 0, 0:T], start=True, stop=False,
                                 skip_group_check=True)
            a.per = 6
            with pe.Fori(0, NJ // 2) as jp:
                a.enter(jp)
                for b in range(2):
                    dst = fill_a()
                    for m in range(KT):
                        mm = nc.tensor.matmul(dst[:, 0:P], wfc1[:, m, b * P:(b + 1) * P], winT[:, m, bass.ds(jp * P, P)],
                                              start=(m == 0), stop=(m == KT - 1))
                    mm.then_inc(a_full, 1)
                    pe.wait_ge(xn_ready, jp * 2 + b + 1)
                    dst = fill_a()
                    for f in range(FT):
                        mm = nc.tensor.transpose(dst[:, f * P:(f + 1) * P], xj[:, b, f * P:(f + 1) * P], ident[:])
                    mm.then_inc(a_full, 1)
                    turned = a.value()
                    dst = fill_a()
                    wait_a(turned)
                    for f in range(FT):
                        mm = nc.tensor.matmul(dst[:, 0:C], xnT[:, b, f * P:(f + 1) * P], gnn_w[:, f, :],
                                              start=(f == 0), stop=(f == FT - 1))
                    mm.then_inc(a_full, 1)
                    wait_a(a.value())
                    pe.wait_ge(adj0_landed[b], (jp + 1) * 16)
                    for f in range(FT):
                        mm = nc.tensor.matmul(bank_g[f][:], xws[:, b, f * P:(f + 1) * P], adj_r[:, b, :],
                                              start=False, stop=False, skip_group_check=True)
                    mm.then_inc(adj_free, 1)
                a.leave(NJ // 2)
            for f in range(FT):
                mm = nc.tensor.matmul(bank_g[f][:], state[:].rearrange("p s i -> p (s i)"), winT[:, 0, 0:T], start=False,
                                      stop=True, skip_group_check=True)
            mm.then_inc(adj_free, 1)
            a.per = A_PER
            pe.wait_ge(dve_const, 1 + 4 * CT)

            def gnn_product(k, v):
                j, f = v // FT, v % FT
                s = j % ADJ_SLOTS
                if f == 0:
                    pe.wait_ge(adj_landed[s], ((k - 1) * (NJ // ADJ_SLOTS) + j // ADJ_SLOTS + 1) * 32)
                    if j == 0:
                        pe.wait_ge(g_taken, (k + 1) * FT)
                mm = nc.tensor.matmul(bank_g[f][:], xw_r[:, s, f * P:(f + 1) * P], adj_r[:, s, :],
                                      start=(j == 0), stop=(j == NJ - 1))
                if f == FT - 1:
                    mm.then_inc(adj_free, 1)

            def gnn_turn(k, h):
                pe.wait_ge(g_taken, (k + 2) * FT)
                dst = fill_d()
                for b in range(2):
                    for f in range(FT):
                        c = (2 * h + b) * P
                        mm = nc.tensor.transpose(dst[:, b * C + f * P:b * C + (f + 1) * P], gT[:, f, c:c + P], ident[:])
                mm.then_inc(d_full, 1)

            def xln_turn(k, f):
                pe.wait_ge(xln_ready, (k + 1) * TB)
                dst = fill_a()
                for b in range(TB):
                    mm = nc.tensor.transpose(dst[:, b * P:(b + 1) * P], xin[:, b, f * P:(f + 1) * P], ident[:])
                mm.then_inc(a_full, 1)

            def in_product(k, c):
                dst = fill_a()
                for f in range(FT):
                    mm = nc.tensor.matmul(dst[:], win_c[:, f, c * P:(c + 1) * P],
                                          xlnT[:, bass.ds((k % 2) * FT + f, 1), :].rearrange("p o t -> p (o t)"),
                                          start=(f == 0), stop=(f == FT - 1))
                mm.then_inc(a_full, 1)

            def conv(i, half):
                if half == 0:
                    fill_a()
                    wait_a(a.value() - 1)
                dst = bank_a[(a.n - 1) % 2]
                for w in (2 * half, 2 * half + 1):
                    mm = nc.tensor.matmul(dst[:], diag[:, i, w, :], upre[:, i % 2, w:w + T], start=(w == 0), stop=(w == 3))
                if half:
                    mm.then_inc(a_full, 1)

            def dbc_product(k, part):
                if part == 0:
                    fill_a()
                dst = bank_a[(a.n - 1) % 2]
                for i in (2 * part, 2 * part + 1):
                    pe.wait_ge(silu_u, k * CT + i + 1)
                    mm = nc.tensor.matmul(dst[:], wx[:, i, :], u[:, i, :], start=(i == 0), stop=(i == CT - 1))
                if part == 3:
                    mm.then_inc(a_full, 1)

            def c_turn():
                dst = fill_a()
                wait_a(a.value() - 1)
                for b in range(TB):
                    mm = nc.tensor.transpose(dst[:, b * P:(b + 1) * P], dbc[:, b * P:(b + 1) * P], ident[:])
                mm.then_inc(a_full, 1)

            def dt_product(i):
                dst = fill_a()
                nc.tensor.matmul(dst[:], wdt[:, i * P:(i + 1) * P], dbc[:], start=True, stop=True).then_inc(a_full, 1)

            def turn_h(k, g, r, b):
                n = g * STEPS + r
                if b == 0:
                    if r == 0:
                        pe.wait_ge(skip_ready, k * CT + (g + 1) * G)
                    else:
                        pe.wait_ge(scanned, k * UNITS + (g * NS + r) * G + SCAN_FREE)
                pe.wait_ge(t_free, k * T_PER + n * TB + b + 1)
                for q in range(G):
                    mm = nc.tensor.transpose(bank_t[b % 2][:, q * P:(q + 1) * P], hbuf[:, n % 2, q, b * P:(b + 1) * P], ident[:])
                mm.then_inc(t_full, 1)

            def turn_y(k, g):
                for b in range(TB):
                    pe.wait_ge(t_free, k * T_PER + ((g + 1) * STEPS - 1) * TB + b + 1 + FREE)
                    dst = fill_d()
                    for q in range(G):
                        mm = nc.tensor.transpose(dst[:, q * P:(q + 1) * P], yT[:, b, q * P:(q + 1) * P], ident[:])
                    mm.then_inc(d_full, 1)

            def out_product(g, b, after):
                if b % 2 == 0:
                    fill_d()
                dst = bank_d[(d.n - 1) % 2]
                gated = d.value() - b // 2 - 1 - (TB - 1 - b) - after
                pe.wait_ge(d_free, gated + FREE)
                for q in range(G):
                    mm = nc.tensor.matmul(dst[:, (b % 2) * C:(b % 2 + 1) * C], zs[:, q, b * P:(b + 1) * P], wout_c[:, g * G + q, :],
                                          start=(q == 0), stop=(q == G - 1))
                if b % 2:
                    mm.then_inc(d_full, 1)

            def beside(k, x, first, last):
                if x in OUT_AT and not first:
                    out_product(1, OUT_AT.index(x), 0)
                if x in DT_HIGH_AT:
                    dt_product(G + DT_HIGH_AT.index(x))
                if x in Z_LOW_AT:
                    in_product(k, CT + Z_LOW_AT.index(x))
                if x in OUT_LOW_AT:
                    out_product(0, OUT_LOW_AT.index(x), 0)
                if x in Z_HIGH_AT:
                    in_product(k, CT + G + Z_HIGH_AT.index(x))
                if last:
                    return
                for v in range(2 * NJ):
                    if GNN_AT[v] == x:
                        gnn_product(k + 1, v)
                if x in GT_AT:
                    gnn_turn(k + 1, GT_AT.index(x))
                if x in XLN_AT:
                    xln_turn(k + 1, XLN_AT.index(x))
                if x in IN_AT:
                    if x == IN_AT[0]:
                        wait_a(a.value())
                    in_product(k + 1, IN_AT.index(x))
                if x in CONV_AT:
                    conv(CONV_AT.index(x), 0)
                if x - 1 in CONV_AT:
                    conv(CONV_AT.index(x - 1), 1)
                if x in DBC_AT:
                    dbc_product(k + 1, DBC_AT.index(x))
                if x == C_AT:
                    c_turn()
                if x in DT_LOW_AT:
                    dt_product(DT_LOW_AT.index(x))

            def chunk(k, first=False, last=False):
                for g in range(NG):
                    if g:
                        turn_y(k, 0)
                    elif not first:
                        turn_y(k - 1, 1)
                    for r in range(STEPS):
                        for b in range(TB):
                            turn_h(k, g, r, b)
                            beside(k, (g * STEPS + r) * TB + b, first, last)

            for h in range(TB // 2):
                gnn_turn(0, h)
            for f in range(FT):
                xln_turn(0, f)
            wait_a(a.value())
            for i in range(CT):
                in_product(0, i)
                for half in range(2):
                    conv(i, half)
            for part in range(4):
                dbc_product(0, part)
            c_turn()
            for i in range(G):
                dt_product(i)
            chunk(0, first=True)
            with pe.Fori(1, NCH - 1) as k:
                a.enter(k - 1)
                d.enter(k - 1)
                chunk(k)
                a.leave(NCH - 2)
                d.leave(NCH - 2)
            chunk(NCH - 1, last=True)
            turn_y(NCH - 1, 1)
            for b in range(TB):
                out_product(1, b, 0)

        @block.vector
        def _(dve):
            d = Tally(D_PER)
            me = Tally(2 * TB + TB // 2 + TB)

            def take():
                dve.wait_ge(d_full, d.next() + 1)
                return bank_d[(d.n - 1) % 2]

            dve.sem_inc(d_free, FREE)
            dve.sem_inc(t_free, FREE)
            dve.sem_inc(scanned, SCAN_FREE)
            dve.sem_inc(rows_free, 2)
            dve.wait_ge(act_const, 1)
            nc.vector.tensor_scalar(amat[:], amat[:], -1.0, None, ALU.mult).then_inc(dve_const, 1)
            dve.wait_ge(const_landed, CONST_ALL)
            dve.wait_ge(pool_const, 7)
            for i in range(CT):
                for w in range(4):
                    nc.vector.tensor_scalar(diag[:, i, w, :], ident[:], convw[:, i, w:w + 1], None, ALU.mult).then_inc(dve_const, 1)
            me.per = 2 * 2
            with dve.Fori(0, NJ // 2) as jp:
                me.enter(jp)
                for b in range(2):
                    dve.wait_ge(rows_landed[b], (jp + 1) * 16)
                    nc.vector.reduce_sum(stat[:, b, 0:1], rows[:, b, :], AX_X).then_inc(rows_free, 1)
                    dve.wait_ge(rows_free, jp * 2 + b + 3)
                    dve.wait_ge(xj_landed[b], (jp + 1) * 16)
                    nc.vector.bn_stats(st[:, b, :], xj[:, b, :]).then_inc(dve_self, 1)
                    dve.wait_ge(dve_self, me.next())
                    nc.vector.tensor_scalar(stat[:, b, 0:1], stat[:, b, 0:1], 1.0, None, ALU.add)
                    nc.vector.bn_aggr(mv[:, b, :], st[:, b, :]).then_inc(dve_self, 1)
                    dve.wait_ge(dve_self, me.next())
                    nc.vector.tensor_scalar(stat[:, b, 1:2], mv[:, b, 1:2], EPS, None, ALU.add).then_inc(stat_ready, 1)
                    dve.wait_ge(pow_done, jp * 2 + b + 1)
                    nc.vector.tensor_scalar(xj[:, b, :], xj[:, b, :], mv[:, b, 0:1], srstd[:, b:b + 1],
                                            ALU.subtract, ALU.mult).then_inc(xn_ready, 1)
                me.leave(NJ // 2)
            me.per = 2 * TB + TB // 2 + TB

            def x1_pair(k, h):
                if h == 0:
                    dve.wait_ge(x_landed, (k + 1) * 32)
                pair = slice(2 * h, 2 * h + 2)
                src = take()
                nc.vector.tensor_tensor(x1[:, pair, :], src[:].rearrange("p (b c) -> p b c", b=2), xwi[:, pair, :],
                                        ALU.add).then_inc(d_free, 1)
                dve.wait_ge(d_free, d.value() + FREE)
                for b in range(2 * h, 2 * h + 2):
                    nc.vector.scalar_tensor_tensor(x1[:, b, :], x1[:, b, :], dinv[:, bass.ds(k * TB + b, 1)], gnn_b[:],
                                                   ALU.mult, ALU.add).then_inc(dve_self, 1)
                    v = me.next()
                dve.wait_ge(dve_self, v)
                nc.vector.scalar_tensor_tensor(x1[:, pair, :], x1[:, pair, :], 0.0, xin[:, pair, :],
                                               ALU.max, ALU.add).then_inc(dve_self, 1)
                dve.wait_ge(dve_self, me.next())
                for b in range(2 * h, 2 * h + 2):
                    nc.vector.bn_stats(st[:, b, :], x1[:, b, :]).then_inc(dve_self, 1)
                    if b:
                        nc.vector.bn_aggr(mv[:, b - 1, :], st[:, b - 1, :]).then_inc(dve_self, 1)
                        me.next()
                    dve.wait_ge(dve_self, me.next())

            def variance():
                last = TB - 1
                nc.vector.tensor_scalar(mv[:, 0:last, 1], mv[:, 0:last, 1], EPS, None, ALU.add)
                nc.vector.bn_aggr(mv[:, last, :], st[:, last, :]).then_inc(dve_self, 1)
                dve.wait_ge(dve_self, me.next())
                nc.vector.tensor_scalar(mv[:, last, 1:2], mv[:, last, 1:2], EPS, None, ALU.add).then_inc(var_ready, 1)

            def xln(k):
                dve.wait_ge(rstd_ready, k + 1)
                for b in range(TB):
                    nc.vector.tensor_scalar(xin[:, b, :], x1[:, b, :], mv[:, b, 0:1], rstd[:, b:b + 1],
                                            ALU.subtract, ALU.mult).then_inc(xln_ready, 1)

            def scan(k, g, s, q):
                unit = (g * NS + s) * G + q
                n = g * STEPS + s + 1
                if q == 0:
                    dve.wait_ge(t_full, k * T_PER + n * TB)
                    dve.wait_ge(saved, (k + 1) * (NG * NS) + g * NS + max(s - 1, 0))
                dve.wait_ge(decay_ready, k * UNITS + unit + 1)
                dve.wait_ge(drive_ready, k * UNITS + unit + 1 + DRIVE_FREE)
                nc.vector.tensor_tensor_scan(hbuf[:, n % 2, q, :], decay[:, unit % DEC_SLOTS, :], drive[:, unit % DRV_SLOTS, :],
                                             state[:, s, g * G + q:g * G + q + 1], ALU.mult, ALU.add).then_inc(scanned, 1)

            def add_up(k, g, r, b):
                use = k * T_PER + (g * STEPS + r) * TB + b
                dve.wait_ge(t_full, use + 1 + TB)
                if r == 0:
                    nc.vector.tensor_copy(yT[:, b, :], bank_t[b % 2][:]).then_inc(t_free, 1)
                else:
                    dve.wait_ge(t_free, use - TB + 1 + FREE)
                    nc.vector.scalar_tensor_tensor(yT[:, b, :], bank_t[b % 2][:], ccol[:, bass.ds(k * TB + b, 1), r - 1],
                                                   yT[:, b, :], ALU.mult, ALU.add).then_inc(t_free, 1)

            def gate(k, g, b):
                if b == 0:
                    dve.wait_ge(silu_z, k * CT + (g + 1) * G)
                src = take()
                part = zs[:, :, b * P:(b + 1) * P]
                nc.vector.tensor_tensor(part, src[:].rearrange("p (q t) -> p q t", q=G), part, ALU.mult).then_inc(d_free, 1)

            def add_out(k, h):
                if h == 0:
                    dve.wait_ge(xo_ready, (k + 1) * TB)
                src = take()
                pair = slice(2 * h, 2 * h + 2)
                nc.vector.tensor_tensor(xo[:, pair, :], src[:].rearrange("p (b c) -> p b c", b=2), xo[:, pair, :],
                                        ALU.add).then_inc(d_free, 1)

            def beside(k, x, first, last):
                for h in range(TB // 2):
                    if x == OUT_AT[2 * h + 1] + 5 and not first:
                        add_out(k - 1, h)
                    if x == OUT_LOW_AT[2 * h + 1] + 5:
                        add_out(k, h)
                    if x == GT_AT[h] + 6 and not last:
                        if h == 0:
                            dve.wait_ge(xo_ready, (k + 1) * TB)
                        x1_pair(k + 1, h)
                        if h:
                            variance()
                if x == (STEPS - 1) * TB + 3 and not last:
                    xln(k + 1)

            def chunk(k, first=False, last=False):
                dve.wait_ge(c_ready, k + 1)
                for g in range(NG):
                    kp, gp = (k, 0) if g else (k - 1, 1)
                    if g or not first:
                        for b in range(TB):
                            add_up(kp, gp, NS, b)
                    for q in range(G):
                        scan(k, g, 0, q)
                    if g or not first:
                        for b in range(TB):
                            gate(kp, gp, b)
                    for b in range(TB):
                        add_up(k, g, 0, b)
                    for s in range(1, NS):
                        for q in range(G):
                            scan(k, g, s, q)
                            add_up(k, g, s, q)
                            beside(k, (g * STEPS + s + 1) * TB + q, first, last)

            for h in range(TB // 2):
                x1_pair(0, h)
            variance()
            xln(0)
            chunk(0, first=True)
            with dve.Fori(1, NCH - 1) as k:
                d.enter(k - 1)
                me.enter(k - 1)
                chunk(k)
                d.leave(NCH - 2)
                me.leave(NCH - 2)
            chunk(NCH - 1, last=True)
            for b in range(TB):
                add_up(NCH - 1, 1, NS, b)
            for b in range(TB):
                gate(NCH - 1, 1, b)
            for h in range(TB // 2):
                add_out(NCH - 1, h)


INPUTS = ("adj", "adjT", "x", "gnn_w", "gnn_b", "wfc1", "bfc1", "winT", "conv_w", "conv_b", "wxT", "wdtT", "b_dt",
          "A_log", "D", "wout", "wfc2T", "b_fc2")


def kernel(x, adj, L0_gnn_W, L0_gnn_b, L0_ffn_W_fc1, L0_ffn_b_fc1, L0_ffn_W_in, L0_ffn_conv_w, L0_ffn_conv_b,
           L0_ffn_W_xproj, L0_ffn_W_dt, L0_ffn_b_dt, L0_ffn_A_log, L0_ffn_D, L0_ffn_W_out, L0_ffn_W_fc2, L0_ffn_b_fc2):
    import concourse.bacc as bacc
    from concourse.bass_utils import run_bass_kernel_spmd

    def by_channel(v):
        v = np.asarray(v)
        w = v.reshape(v.shape[0] // P, P, -1).transpose(1, 0, 2)
        return w if v.ndim > 1 else w[:, :, 0]

    arrays = dict(
        adj=adj, adjT=np.asarray(adj).T, x=x, gnn_w=np.asarray(L0_gnn_W).T, gnn_b=L0_gnn_b, wfc1=L0_ffn_W_fc1,
        bfc1=by_channel(L0_ffn_b_fc1), winT=np.asarray(L0_ffn_W_in).T, conv_w=by_channel(L0_ffn_conv_w),
        conv_b=by_channel(L0_ffn_conv_b), wxT=np.asarray(L0_ffn_W_xproj).T, wdtT=np.asarray(L0_ffn_W_dt).T,
        b_dt=by_channel(L0_ffn_b_dt), A_log=by_channel(L0_ffn_A_log), D=by_channel(L0_ffn_D), wout=L0_ffn_W_out,
        wfc2T=np.asarray(L0_ffn_W_fc2).T, b_fc2=L0_ffn_b_fc2)
    arrays = {"in_" + n: np.ascontiguousarray(arrays[n]) for n in INPUTS}
    nc = bacc.Bacc("TRN2", target_bir_lowering=False, num_devices=1)
    t = {n: nc.dram_tensor("in_" + n, arrays["in_" + n].shape, F32, kind="ExternalInput").ap() for n in INPUTS}
    t["out"] = nc.dram_tensor("out", [N, C], F32, kind="ExternalOutput").ap()
    build(nc, t)
    return run_bass_kernel_spmd(nc, [arrays], core_ids=[0]).results[0]["out"]
```

```python
from contextlib import ExitStack

import numpy as np

import concourse.bass as bass
from concourse import mybir

F32 = mybir.dt.float32
ACT = mybir.ActivationFunctionType
ALU = mybir.AluOpType
AX_X = mybir.AxisListType.X

P = 128
N = 4096
C = 256
DM = 512
DI = 1024
NS = 16
R = 32
T = 512
NCH = N // T
TB = T // P
CT = DI // P
G = 4
NG = CT // G
FT = C // P
KT = DM // P
NJ = N // P
STEPS = NS + 1
EPS = 1e-5
ADJ_SLOTS = 4
SETUP_SLOTS = 4
DEC_SLOTS = 4
DRV_SLOTS = 4
B_SLOTS = 4
FREE = 2


class Tally:

    def __init__(self, per=0):
        self.per, self.n, self.base = per, 0, 0

    def next(self):
        self.n += 1
        return self.base + self.n

    def value(self):
        return self.base + self.n

    def enter(self, k):
        self.start, self.base = self.n, k * self.per

    def leave(self, times):
        assert self.n - self.start == self.per, (self.n - self.start, self.per)
        self.n, self.base = self.start + times * self.per, 0


UNITS = NG * NS * G
SCAN_FREE = DEC_SLOTS
DRIVE_FREE = B_SLOTS * G

ACT_LAG = 9
Y_AT = [[0, 1], [2], [3]]
OUT_AT = [6, 8, 10, 12]
DT_HIGH_AT = [14, 20, 26, 32]
GNN_END = 14
GT_AT = [16, 17]
Z_LOW_AT = [18, 19, 22, 24]
XLN_AT = [29, 30]
IN_AT = [34, 40, 45, 50, 62, 69, 75, 82]
CONV_AT = [38, 43, 48, 53, 66, 72, 79, 86]
OUT_LOW_AT = [74, 77, 81, 84]
Z_HIGH_AT = [88, 90, 92, 94]
DBC_AT = [99, 101, 103, 105]
C_AT = 108
DT_LOW_AT = [110, 115, 120, 125]
GNN_EARLY = [0, 1, 2, 3, 4, 5, 7, 9, 11, 13]
GNN_LATE = list(range(20, 34)) + [36, 42, 47] + list(range(55, 62)) + [95, 96, 97, 98, 100, 102, 104, 106, 107] + \
    [x for x in range(109, 134) if x not in DT_LOW_AT]
NLATE = len(GNN_LATE)
assert NLATE % 2 == 0 and NLATE + len(GNN_EARLY) == 2 * NJ, NLATE
X1_AT = [21 + i for i in range(TB // 2 * 4)]
LN_AT = 31
RSTD_AT = 33
XO_AT = 8
SILU_LOW_AT = CONV_AT[3] + 1 + ACT_LAG
SILU_HIGH_AT = Z_HIGH_AT[-1] + 1 + ACT_LAG
TILE_AT = GNN_EARLY[0::2] + GNN_LATE[0::2]
ADJ_BY = [0] + [sum(x <= 4 * j + 12 for x in TILE_AT) for j in range(NG * NS)]
ADJ_BY[-1] = NJ

A_PER = 2 + CT + CT + 1 + 1 + CT + CT
D_GROUP = TB + TB // 2
D_PER = 2 + NG * D_GROUP
T_PER = NG * STEPS * TB


def build(nc, t):
    nc.disable_value_cache = True
    ctx = ExitStack()
    with ctx:
        def sb(name, *shape):
            return ctx.enter_context(nc.sbuf_tensor(name, [P, *shape], F32))

        def sem(name):
            return ctx.enter_context(nc.semaphore(name))

        xw_dram = nc.dram_tensor("xw_scratch", [N, C], F32, kind="Internal").ap()
        b_dram = nc.dram_tensor("b_scratch", [NCH, NS, T], F32, kind="Internal").ap()

        win_c = sb("win_c", FT, 2 * DI)
        wout_c = sb("wout_c", CT, C)
        wx = sb("wx", CT, P)
        wdt = sb("wdt", DI)
        diag = sb("diag", CT, 4, P)
        ident = sb("ident", P)
        bin_c = sb("bin_c", 2 * CT)
        convw = sb("convw", CT, 4)
        convb = sb("convb", CT)
        bdt = sb("bdt", CT)
        dpar = sb("dpar", CT)
        amat = sb("amat", CT, NS)
        gnn_b = sb("gnn_b", C)
        fc2_b = sb("fc2_b", C)
        mhalf = sb("mhalf", TB)
        dinv = sb("dinv", NJ)
        adj_r = sb("adj_r", ADJ_SLOTS, T)
        xw_r = sb("xw_r", ADJ_SLOTS, C)
        xin = sb("xin", TB, C)
        xwi = sb("xwi", TB, C)
        x1 = sb("x1", TB, C)
        mv = sb("mv", TB, 2)
        st = sb("st", TB, 6)
        rstd = sb("rstd", TB)
        xlnT = sb("xlnT", 2 * FT, T)
        xo = sb("xo", 2, TB, C)
        upre = sb("upre", 2, T + 3)
        hist = sb("hist", CT, 3)
        dbc = sb("dbc", T)
        ccol = sb("ccol", NCH * TB, NS)
        bcast = sb("bcast", B_SLOTS, T)
        state = sb("state", NS, CT)
        yT = sb("yT", TB, G * P)
        big = sb("big", 14336)
        u = big[:, 0:4096].rearrange("p (i t) -> p i t", t=T)
        hbuf = big[:, 4096:8192].rearrange("p (b q t) -> p b q t", b=2, t=T)
        decay = big[:, 8192:10240].rearrange("p (b t) -> p b t", t=T)
        du = big[:, 10240:14336].rearrange("p (i t) -> p i t", t=T)
        big2 = sb("big2", 8192)
        delta = big2[:, 0:4096].rearrange("p (i t) -> p i t", t=T)
        zs = big2[:, 4096:6144].rearrange("p (q t) -> p q t", t=T)
        drive = big2[:, 6144:8192].rearrange("p (b t) -> p b t", t=T)
        winT = big[:, 0:8192].rearrange("p (m e) -> p m e", m=KT)
        woutM = big[:, 8192:12288].rearrange("p (m d) -> p m d", m=KT)
        wfc1 = big[:, 12288:13312].rearrange("p (m f) -> p m f", m=KT)
        wfc2T = big[:, 13312:14336].rearrange("p (m o) -> p m o", m=KT)
        gnn_w = yT[:, 0, :].rearrange("p (f o) -> p f o", f=FT)
        bfc1 = yT[:, 1, 0:KT]
        rows = big2[:, :].rearrange("p (b n) -> p b n", b=2)
        xj, xws, xnT = xin, x1, xwi
        stat = sb("stat", SETUP_SLOTS, 2)
        srstd = sb("srstd", SETUP_SLOTS)
        gT = upre[:, :, 0:T]

        def bank(name):
            return ctx.enter_context(nc.psum_tensor(name, [P, 512], F32))
        bank_a = [bank(f"bank_a{i}") for i in range(2)]
        bank_d = [bank(f"bank_d{i}") for i in range(2)]
        bank_t = [bank(f"bank_t{i}") for i in range(2)]
        bank_g = [bank(f"bank_g{i}") for i in range(FT)]

        const_landed = sem("const_landed")
        pool_const = sem("pool_const")
        dve_const = sem("dve_const")
        act_const = sem("act_const")
        rows_landed = [sem(f"rows_landed{i}") for i in range(2)]
        stat_ready = sem("stat_ready")
        pow_done = sem("pow_done")
        xn_ready = sem("xn_ready")
        xj_landed = [sem(f"xj_landed{i}") for i in range(SETUP_SLOTS)]
        adj0_landed = [sem(f"adj0_landed{i}") for i in range(SETUP_SLOTS)]
        rows_free = sem("rows_free")
        xw_stored = [sem(f"xw_stored{i}") for i in range(SETUP_SLOTS)]
        a_full = sem("a_full")
        a_free = sem("a_free")
        d_full = sem("d_full")
        d_free = sem("d_free")
        t_full = sem("t_full")
        t_free = sem("t_free")
        adj_landed = [sem(f"adj_landed{i}") for i in range(ADJ_SLOTS)]
        adj_free = sem("adj_free")
        g0_closed = sem("g0_closed")
        g_taken = sem("g_taken")
        x_landed = sem("x_landed")
        xo_ready = sem("xo_ready")
        var_ready = sem("var_ready")
        rstd_ready = sem("rstd_ready")
        xln_ready = sem("xln_ready")
        dve_self = sem("dve_self")
        act_self = sem("act_self")
        hist_saved = sem("hist_saved")
        skip_ready = sem("skip_ready")
        silu_u = sem("silu_u")
        silu_z = sem("silu_z")
        c_ready = sem("c_ready")
        b_stored = sem("b_stored")
        b_landed = [sem(f"b_landed{i}") for i in range(B_SLOTS)]
        soft_ready = sem("soft_ready")
        delta_ready = sem("delta_ready")
        du_ready = sem("du_ready")
        decay_ready = sem("decay_ready")
        drive_ready = sem("drive_ready")
        scanned = sem("scanned")
        saved = sem("saved")
        out_stored = sem("out_stored")

        block = ctx.enter_context(nc.Block())

        CONSTS = [
            (winT, t["winT"].rearrange("(m p) e -> p m e", p=P)),
            (wfc1, t["wfc1"].rearrange("(m p) f -> p m f", p=P)),
            (bfc1, t["bfc1"]),
            (woutM, t["wout"].rearrange("(m p) d -> p m d", p=P)),
            (wfc2T, t["wfc2T"].rearrange("(m p) o -> p m o", p=P)),
            (gnn_w, t["gnn_w"].rearrange("(f p) o -> p f o", p=P)),
            (convw[:], t["conv_w"]), (convb[:], t["conv_b"]), (bdt[:], t["b_dt"]), (dpar[:], t["D"]),
            (amat[:], t["A_log"]),
            (gnn_b[:], t["gnn_b"].partition_broadcast(P)), (fc2_b[:], t["b_fc2"].partition_broadcast(P)),
        ]
        PADDED = [
            (wx[:, :, 0:R + 2 * NS], t["wxT"].rearrange("(i p) e -> p i e", p=P)),
            (wdt[0:R, :], t["wdtT"]),
        ]
        CONST_ALL = 16 * (len(CONSTS) + len(PADDED))

        @block.sync
        def _(sp):
            sp.sem_inc(out_stored, 32)
            for dst, src in CONSTS:
                sp.dma_start(dst, src).then_inc(const_landed, 16)
            sp.wait_ge(pool_const, 2)
            for dst, src in PADDED:
                sp.dma_start(dst, src).then_inc(const_landed, 16)
            with sp.Fori(0, NJ // SETUP_SLOTS) as jp:
                for b in range(SETUP_SLOTS):
                    j = jp * SETUP_SLOTS + b
                    sp.wait_ge(rows_free, j + 1)
                    sp.dma_start(rows[:, b % 2, :], t["adj"][bass.ds(j * P, P), :]).then_inc(rows_landed[b % 2], 16)
                    sp.wait_ge(adj_free, j + 1)
                    sp.dma_start(xj[:, b, :], t["x"][bass.ds(j * P, P), :]).then_inc(xj_landed[b], 16)
                    sp.dma_start(adj_r[:, b, :], t["adjT"][bass.ds(j * P, P), 0:T]).then_inc(adj0_landed[b], 16)
            for b in range(SETUP_SLOTS):
                sp.wait_ge(xw_stored[b], 16 * (NJ // SETUP_SLOTS + 1))
            sp.wait_ge(adj_free, NJ + ADJ_SLOTS)

            def load_own(c):
                sp.dma_start(xin[:], t["x"][bass.ds(c * T, T), :].rearrange("(b p) c -> p b c", p=P)).then_inc(x_landed, 16)
                sp.dma_start(xwi[:], xw_dram[bass.ds(c * T, T), :].rearrange("(b p) c -> p b c", p=P)).then_inc(x_landed, 16)

            def load_adj(c, j):
                s = j % ADJ_SLOTS
                sp.wait_ge(adj_free, c * NJ + j + 1)
                sp.dma_start(adj_r[:, s, :], t["adjT"][j * P:(j + 1) * P, bass.ds(c * T, T)]).then_inc(adj_landed[s], 16)
                sp.dma_start(xw_r[:, s, :], xw_dram[j * P:(j + 1) * P, :]).then_inc(adj_landed[s], 16)

            def load_b(c, step):
                sp.wait_ge(drive_ready, c * UNITS + (step + 1 - B_SLOTS) * G + DRIVE_FREE)
                sp.dma_start(bcast[:, step % B_SLOTS, :],
                             b_dram[bass.ds(c, 1), step % NS, :].partition_broadcast(P)).then_inc(b_landed[step % B_SLOTS], 16)

            def store_out(c, last=False):
                sp.wait_ge(d_free, (c + 1) * D_PER + (0 if last else 2) + FREE)
                sp.dma_start(t["out"][bass.ds(c * T, T), :].rearrange("(b p) c -> p b c", p=P),
                             xo[:, bass.ds(c % 2, 1)].rearrange("p o b c -> p (o b) c")).then_inc(out_stored, 16)

            def chunk(k, first=False, last=False, pre=True):
                if not last:
                    sp.wait_ge(silu_u, (k + 1) * CT)
                    load_own(k + 1)
                for j in range(NG * NS):
                    if not last:
                        for i in range(ADJ_BY[j], ADJ_BY[j + 1]):
                            if i < NJ - NLATE // 2:
                                load_adj(k + 1, NLATE // 2 + i)
                            elif pre:
                                load_adj(k + 2, i - (NJ - NLATE // 2))
                        if j == NG * NS - B_SLOTS:
                            sp.wait_ge(b_stored, (k + 3) * 16)
                    if j + B_SLOTS < NG * NS:
                        load_b(k, j + B_SLOTS)
                    elif not last:
                        load_b(k + 1, j + B_SLOTS - NG * NS)
                    if j == 6 and not first:
                        store_out(k - 1)

            load_own(0)
            for j in range(NLATE // 2):
                load_adj(1, j)
            sp.wait_ge(b_stored, 2 * 16)
            for step in range(B_SLOTS):
                load_b(0, step)
            chunk(0, first=True)
            with sp.Fori(1, NCH - 2) as k:
                chunk(k)
            chunk(NCH - 2, pre=False)
            chunk(NCH - 1, last=True)
            store_out(NCH - 1, last=True)
            sp.wait_ge(out_stored, 16 * (NCH + 2))

        @block.gpsimd
        def _(pool):
            nc.gpsimd.memset(wx[:], 0.0).then_inc(pool_const, 1)
            nc.gpsimd.memset(wdt[:], 0.0).then_inc(pool_const, 1)
            nc.gpsimd.memset(mhalf[:], -0.5).then_inc(pool_const, 1)
            nc.gpsimd.memset(state[:], 0.0).then_inc(pool_const, 1)
            nc.gpsimd.memset(hist[:], 0.0).then_inc(pool_const, 1)
            nc.gpsimd.memset(ident[:], 0.0).then_inc(pool_const, 1)
            pool.wait_ge(pool_const, 6)
            nc.gpsimd.affine_select(out=ident[:], in_=ident[:], compare_op=ALU.not_equal, fill=1.0, base=0,
                                    pattern=[[-1, P]], channel_multiplier=1).then_inc(pool_const, 1)
            with pool.Fori(0, NJ // SETUP_SLOTS) as jp:
                for b in range(SETUP_SLOTS):
                    j = jp * SETUP_SLOTS + b
                    pool.wait_ge(stat_ready, j + 1)
                    nc.gpsimd.tensor_tensor(srstd[:, b:b + 1], stat[:, b, 1:2], mhalf[:, 0:1], ALU.pow)
                    nc.gpsimd.tensor_tensor(dinv[:, bass.ds(j, 1)], stat[:, b, 0:1], mhalf[:, 0:1],
                                            ALU.pow).then_inc(pow_done, 1)
            pool.sem_inc(drive_ready, DRIVE_FREE)
            pool.sem_inc(du_ready, CT)

            def rstd_of(c):
                pool.wait_ge(var_ready, c + 1)
                nc.gpsimd.tensor_tensor(rstd[:], mv[:, :, 1], mhalf[:], ALU.pow).then_inc(rstd_ready, 1)

            def start_out(k):
                pool.wait_ge(out_stored, k * 16 + 16)
                pool.wait_ge(xln_ready, (k + 1) * TB)
                for b in range(TB):
                    nc.gpsimd.tensor_tensor(xo[:, bass.ds(k % 2, 1), b, :].rearrange("p o c -> p (o c)"), x1[:, b, :], fc2_b[:],
                                            ALU.add).then_inc(xo_ready, 1)

            def delta_du(c, i):
                pool.wait_ge(soft_ready, c * CT + i + 1)
                nc.gpsimd.tensor_tensor(delta[:, i, :], delta[:, i, :], du[:, i, :], ALU.add).then_inc(delta_ready, 1)
                pool.wait_ge(delta_ready, c * CT + i + 1)
                nc.gpsimd.tensor_tensor(du[:, i, :], delta[:, i, :], u[:, i, :], ALU.mult).then_inc(du_ready, 1)

            def drive_of(k, g, s, q):
                unit = (g * NS + s) * G + q
                if q == 0:
                    pool.wait_ge(b_landed[s % B_SLOTS], (k * (NG * NS // B_SLOTS) + (g * NS + s) // B_SLOTS + 1) * 16)
                if s == 0:
                    pool.wait_ge(du_ready, (k + 1) * CT + g * G + q + 1)
                pool.wait_ge(scanned, k * UNITS + unit + 1 - DRV_SLOTS + SCAN_FREE)
                nc.gpsimd.tensor_tensor(drive[:, unit % DRV_SLOTS, :], du[:, g * G + q, :], bcast[:, s % B_SLOTS, :],
                                        ALU.mult).then_inc(drive_ready, 1)

            def chunk(k, last=False):
                for g in range(NG):
                    for s in range(NS):
                        for q in range(G):
                            x = (g * STEPS + s + 1) * TB + q
                            if x == RSTD_AT and not last:
                                rstd_of(k + 1)
                            drive_of(k, g, s, q)
                            if x - 1 - ACT_LAG in DT_HIGH_AT:
                                delta_du(k, G + DT_HIGH_AT.index(x - 1 - ACT_LAG))
                            if x - 1 - ACT_LAG in DT_LOW_AT and not last:
                                delta_du(k + 1, DT_LOW_AT.index(x - 1 - ACT_LAG))
                            if x == XO_AT:
                                start_out(k)

            rstd_of(0)
            for i in range(G):
                delta_du(0, i)
            chunk(0)
            with pool.Fori(1, NCH - 1) as k:
                chunk(k)
            chunk(NCH - 1, last=True)

        @block.scalar
        def _(act):
            a = Tally(A_PER)

            def take():
                act.wait_ge(a_full, a.next())
                return bank_a[(a.n - 1) % 2]

            def wait_taken():
                act.wait_ge(a_free, a.value() + FREE)

            act.sem_inc(a_free, FREE)
            act.sem_inc(saved, NG * NS)
            act.sem_inc(hist_saved, CT)
            act.sem_inc(b_stored, 16)
            for b in range(SETUP_SLOTS):
                act.sem_inc(xw_stored[b], 16)
            act.sem_inc(g_taken, FT)
            act.wait_ge(const_landed, CONST_ALL)
            nc.scalar.activation(amat[:], amat[:], ACT.Exp).then_inc(act_const, 1)
            src = take()
            nc.scalar.activation(bin_c[:], src[:, 0:2 * CT], ACT.Copy).then_inc(a_free, 1)
            for i in range(CT):
                src = take()
                nc.scalar.activation(wout_c[:, i, :], src[:, 0:C], ACT.Copy).then_inc(a_free, 1)
            a.per = SETUP_SLOTS * 3
            with act.Fori(0, NJ // SETUP_SLOTS) as jp:
                a.enter(jp)
                for b in range(SETUP_SLOTS):
                    j = jp * SETUP_SLOTS + b
                    src = take()
                    nc.scalar.activation(win_c[:, b % FT, bass.ds((jp * 2 + b // FT) * P, P)], src[:, 0:P], ACT.Copy).then_inc(a_free, 1)
                    src = take()
                    nc.scalar.activation(xnT[:, b, :], src[:, 0:C], ACT.Copy).then_inc(a_free, 1)
                    src = take()
                    act.wait_ge(pow_done, j + 1)
                    act.wait_ge(xw_stored[b], (jp + 1) * 16)
                    act.wait_ge(adj_free, j + 1)
                    nc.scalar.activation(xws[:, b, :], src[:, 0:C], ACT.Copy,
                                         scale=dinv[:, bass.ds(j, 1)]).then_inc(a_free, 1)
                    wait_taken()
                    act.dma_start(xw_dram[bass.ds(j * P, P), :], xws[:, b, :]).then_inc(xw_stored[b], 16)
                a.leave(NJ // SETUP_SLOTS)
            a.per = A_PER
            for b in range(SETUP_SLOTS):
                act.wait_ge(xw_stored[b], 16 * (NJ // SETUP_SLOTS + 1))
            act.wait_ge(dve_const, 1 + 4 * CT)
            me = Tally(2 * CT)

            def gnn_out(k):
                act.wait_ge(adj_free, (k + 1) * NJ + ADJ_SLOTS)
                for f in range(FT):
                    nc.scalar.activation(gT[:, f, :], bank_g[f][:], ACT.Copy).then_inc(g_taken, 1)

            def xln_out(k, f):
                src = take()
                nc.scalar.activation(xlnT[:, bass.ds((k % 2) * FT + f, 1), :].rearrange("p o t -> p (o t)"), src[:],
                                     ACT.Copy).then_inc(a_free, 1)

            def in_out(k, i):
                src = take()
                act.wait_ge(hist_saved, k * CT + i + 1)
                nc.scalar.activation(upre[:, i % 2, 0:3], hist[:, i, :], ACT.Copy)
                nc.scalar.activation(upre[:, i % 2, 3:T + 3], src[:], ACT.Identity, bias=bin_c[:, i:i + 1]).then_inc(a_free, 1)
                wait_taken()
                nc.scalar.activation(hist[:, i, :], upre[:, i % 2, T:T + 3], ACT.Copy).then_inc(hist_saved, 1)

            def conv_out(i):
                src = take()
                nc.scalar.activation(u[:, i, :], src[:], ACT.Identity, bias=convb[:, i:i + 1]).then_inc(a_free, 1)

            def dbc_out(k):
                src = take()
                act.wait_ge(b_stored, (k + 1) * 16)
                nc.scalar.activation(dbc[:], src[:], ACT.Copy).then_inc(a_free, 1)
                wait_taken()
                act.dma_start(b_dram[bass.ds(k, 1)].rearrange("o s t -> (o s) t"), dbc[R:R + NS, :]).then_inc(b_stored, 16)

            def c_out(k):
                src = take()
                nc.scalar.activation(ccol[:, bass.ds(k * TB, TB), :],
                                     src[:].rearrange("p (b e) -> p b e", b=TB)[:, :, R + NS:R + 2 * NS],
                                     ACT.Copy).then_inc(a_free, 1)
                wait_taken()
                act.sem_inc(c_ready, 1)

            def softplus_terms(i):
                src = take()
                nc.scalar.activation(du[:, i, :], src[:], ACT.Abs, bias=bdt[:, i:i + 1]).then_inc(act_self, 1)
                v = me.next()
                nc.scalar.activation(delta[:, i, :], src[:], ACT.Relu, bias=bdt[:, i:i + 1]).then_inc(a_free, 1)
                act.wait_ge(act_self, v)
                nc.scalar.activation(du[:, i, :], du[:, i, :], ACT.Exp, scale=-1.0).then_inc(act_self, 1)
                act.wait_ge(act_self, me.next())
                nc.scalar.activation(du[:, i, :], du[:, i, :], ACT.Ln, bias=1.0).then_inc(soft_ready, 1)

            def z_out(c):
                src = take()
                nc.scalar.activation(zs[:, c % G, :], src[:], ACT.Identity, bias=bin_c[:, CT + c:CT + c + 1]).then_inc(a_free, 1)

            def exp_tables():
                nc.scalar.preload_act_table_set("natural_log_exp_and_others")

            def silu_of_z():
                for q in range(G):
                    nc.scalar.activation(zs[:, q, :], zs[:, q, :], ACT.Silu).then_inc(silu_z, 1)

            def silu_of_u(half):
                for i in range(half * G, (half + 1) * G):
                    nc.scalar.activation(u[:, i, :], u[:, i, :], ACT.Silu).then_inc(silu_u, 1)

            def skip_term(k, g):
                n = g * STEPS
                act.wait_ge(t_full, k * T_PER + n * TB)
                act.wait_ge(saved, (k + 1) * (NG * NS) + g * NS - 1)
                for q in range(G):
                    nc.scalar.activation(hbuf[:, n % 2, q, :], u[:, g * G + q, :], ACT.Copy,
                                         scale=dpar[:, g * G + q:g * G + q + 1]).then_inc(skip_ready, 1)

            def start_y(k, g, b):
                act.wait_ge(t_full, k * T_PER + g * STEPS * TB + b + 1 + TB)
                nc.scalar.activation(yT[:, b, :], bank_t[b % 2][:], ACT.Copy).then_inc(t_free, 1)

            def decay_of(k, g, s, q):
                unit = (g * NS + s) * G + q
                act.wait_ge(scanned, k * UNITS + unit + 1 - DEC_SLOTS + SCAN_FREE)
                nc.scalar.activation(decay[:, unit % DEC_SLOTS, :], delta[:, g * G + q, :], ACT.Exp,
                                     scale=amat[:, g * G + q, s:s + 1]).then_inc(decay_ready, 1)

            def save_state(k, g, s):
                act.wait_ge(scanned, k * UNITS + (g * NS + s + 1) * G + SCAN_FREE)
                nc.scalar.activation(state[:, s, g * G:(g + 1) * G], hbuf[:, (g * STEPS + s + 1) % 2, :, T - 1],
                                     ACT.Copy).then_inc(saved, 1)

            def beside(k, x, first, last):
                y = x - ACT_LAG
                if y in DT_HIGH_AT:
                    if y == DT_HIGH_AT[0]:
                        act.wait_ge(drive_ready, k * UNITS + DRIVE_FREE)
                    softplus_terms(G + DT_HIGH_AT.index(y))
                if y in Z_LOW_AT:
                    if y == Z_LOW_AT[0] and not first:
                        act.wait_ge(d_full, k * D_PER + 2 + 1)
                    z_out(Z_LOW_AT.index(y))
                    if y == Z_LOW_AT[-1]:
                        wait_taken()
                        silu_of_z()
                        exp_tables()
                if y in Z_HIGH_AT:
                    if y == Z_HIGH_AT[0]:
                        act.wait_ge(d_full, k * D_PER + (8 if last else 10) + 1)
                    z_out(G + Z_HIGH_AT.index(y))
                if x == SILU_HIGH_AT and last:
                    wait_taken()
                    silu_of_z()
                    exp_tables()
                if last:
                    return
                if y == GNN_END - 1:
                    gnn_out(k + 1)
                if y in XLN_AT:
                    xln_out(k + 1, XLN_AT.index(y))
                if y in IN_AT:
                    in_out(k + 1, IN_AT.index(y))
                if y - 1 in CONV_AT:
                    if y - 1 == CONV_AT[0]:
                        act.wait_ge(du_ready, (k + 1) * CT + G)
                    if y - 1 == CONV_AT[G]:
                        act.wait_ge(du_ready, (k + 2) * CT)
                        act.wait_ge(skip_ready, (k + 1) * CT)
                    conv_out(CONV_AT.index(y - 1))
                if x == SILU_LOW_AT:
                    wait_taken()
                    silu_of_u(0)
                    exp_tables()
                if x == SILU_HIGH_AT:
                    wait_taken()
                    silu_of_u(1)
                    silu_of_z()
                    exp_tables()
                if y == DBC_AT[-1]:
                    dbc_out(k + 1)
                if y == C_AT:
                    c_out(k + 1)
                if y in DT_LOW_AT:
                    if y == DT_LOW_AT[0]:
                        act.wait_ge(drive_ready, k * UNITS + NS * G + DRIVE_FREE)
                    softplus_terms(DT_LOW_AT.index(y))

            def chunk(k, first=False, last=False):
                for g in range(NG):
                    for r in range(STEPS):
                        for q in range(G):
                            x = (g * STEPS + r) * TB + q
                            if r:
                                if r == 1:
                                    act.wait_ge(delta_ready, k * CT + g * G + q + 1)
                                decay_of(k, g, r - 1, q)
                            if r == 2:
                                start_y(k, g, q)
                            beside(k, x, first, last)
                        if r == 1:
                            if g:
                                save_state(k, 0, NS - 1)
                            elif not first:
                                save_state(k - 1, NG - 1, NS - 1)
                            act.wait_ge(silu_u, (k + 1) * CT)
                            skip_term(k, g)
                        if r > 1:
                            save_state(k, g, r - 2)

            act.wait_ge(g0_closed, 1)
            gnn_out(0)
            for f in range(FT):
                xln_out(0, f)
            for i in range(CT):
                in_out(0, i)
                conv_out(i)
            wait_taken()
            for half in range(2):
                silu_of_u(half)
            exp_tables()
            dbc_out(0)
            c_out(0)
            for i in range(G):
                softplus_terms(i)
            chunk(0, first=True)
            with act.Fori(1, NCH - 1) as k:
                a.enter(k - 1)
                me.enter(k - 1)
                chunk(k)
                a.leave(NCH - 2)
                me.leave(NCH - 2)
            chunk(NCH - 1, last=True)

        @block.tensor
        def _(pe):
            a = Tally(A_PER)
            d = Tally(D_PER)

            def fill_a():
                pe.wait_ge(a_free, a.next())
                return bank_a[(a.n - 1) % 2]

            def fill_d():
                pe.wait_ge(d_free, d.next())
                return bank_d[(d.n - 1) % 2]

            def wait_a(use):
                pe.wait_ge(a_free, use + FREE)

            pe.sem_inc(d_full, 1)
            pe.sem_inc(t_full, TB)
            pe.sem_inc(adj_free, ADJ_SLOTS)
            pe.wait_ge(const_landed, CONST_ALL)
            pe.wait_ge(pool_const, 7)
            dst = fill_a()
            for c in range(2 * CT):
                for m in range(KT):
                    mm = nc.tensor.matmul(dst[:, c:c + 1], winT[:, m, c * P:(c + 1) * P], bfc1[:, m:m + 1],
                                          start=(m == 0), stop=(m == KT - 1))
            mm.then_inc(a_full, 1)
            for i in range(CT):
                dst = fill_a()
                for m in range(KT):
                    mm = nc.tensor.matmul(dst[:, 0:C], woutM[:, m, i * P:(i + 1) * P], wfc2T[:, m, :],
                                          start=(m == 0), stop=(m == KT - 1))
                mm.then_inc(a_full, 1)
            for f in range(FT):
                nc.tensor.matmul(bank_g[f][:], state[:].rearrange("p s i -> p (s i)"), winT[:, 0, 0:T], start=True, stop=False,
                                 skip_group_check=True)
            a.per = SETUP_SLOTS * 3
            with pe.Fori(0, NJ // SETUP_SLOTS) as jp:
                a.enter(jp)
                for b in range(SETUP_SLOTS):
                    j = jp * SETUP_SLOTS + b
                    dst = fill_a()
                    for m in range(KT):
                        mm = nc.tensor.matmul(dst[:, 0:P], wfc1[:, m, (b % FT) * P:(b % FT + 1) * P],
                                              winT[:, m, bass.ds((jp * 2 + b // FT) * P, P)], start=(m == 0), stop=(m == KT - 1))
                    mm.then_inc(a_full, 1)
                    pe.wait_ge(xn_ready, j + 1)
                    dst = fill_a()
                    for f in range(FT):
                        mm = nc.tensor.transpose(dst[:, f * P:(f + 1) * P], xj[:, b, f * P:(f + 1) * P], ident[:])
                    mm.then_inc(a_full, 1)
                    turned = a.value()
                    dst = fill_a()
                    wait_a(turned)
                    for f in range(FT):
                        mm = nc.tensor.matmul(dst[:, 0:C], xnT[:, b, f * P:(f + 1) * P], gnn_w[:, f, :],
                                              start=(f == 0), stop=(f == FT - 1))
                    mm.then_inc(a_full, 1)
                    wait_a(a.value())
                    pe.wait_ge(adj0_landed[b], (jp + 1) * 16)
                    for f in range(FT):
                        mm = nc.tensor.matmul(bank_g[f][:], xws[:, b, f * P:(f + 1) * P], adj_r[:, b, :],
                                              start=False, stop=False, skip_group_check=True)
                    mm.then_inc(adj_free, 1)
                a.leave(NJ // SETUP_SLOTS)
            for f in range(FT):
                mm = nc.tensor.matmul(bank_g[f][:], state[:].rearrange("p s i -> p (s i)"), winT[:, 0, 0:T], start=False,
                                      stop=True, skip_group_check=True)
            mm.then_inc(g0_closed, 1)
            a.per = A_PER
            pe.wait_ge(dve_const, 1 + 4 * CT)

            def gnn_product(k, v):
                j, f = v // FT, v % FT
                s = j % ADJ_SLOTS
                if f == 0:
                    pe.wait_ge(adj_landed[s], ((k - 1) * (NJ // ADJ_SLOTS) + j // ADJ_SLOTS + 1) * 32)
                    if j == 0:
                        pe.wait_ge(g_taken, (k + 1) * FT)
                mm = nc.tensor.matmul(bank_g[f][:], xw_r[:, s, f * P:(f + 1) * P], adj_r[:, s, :],
                                      start=(j == 0), stop=(j == NJ - 1))
                if f == FT - 1:
                    mm.then_inc(adj_free, 1)

            def gnn_turn(k, h):
                pe.wait_ge(g_taken, (k + 2) * FT)
                dst = fill_d()
                for b in range(2):
                    for f in range(FT):
                        c = (2 * h + b) * P
                        mm = nc.tensor.transpose(dst[:, b * C + f * P:b * C + (f + 1) * P], gT[:, f, c:c + P], ident[:])
                mm.then_inc(d_full, 1)

            def xln_turn(k, f):
                pe.wait_ge(xln_ready, (k + 1) * TB)
                dst = fill_a()
                for b in range(TB):
                    mm = nc.tensor.transpose(dst[:, b * P:(b + 1) * P], xin[:, b, f * P:(f + 1) * P], ident[:])
                mm.then_inc(a_full, 1)

            def in_product(k, c):
                dst = fill_a()
                for f in range(FT):
                    mm = nc.tensor.matmul(dst[:], win_c[:, f, c * P:(c + 1) * P],
                                          xlnT[:, bass.ds((k % 2) * FT + f, 1), :].rearrange("p o t -> p (o t)"),
                                          start=(f == 0), stop=(f == FT - 1))
                mm.then_inc(a_full, 1)

            def conv(i, half):
                if half == 0:
                    fill_a()
                    wait_a(a.value() - 1)
                dst = bank_a[(a.n - 1) % 2]
                for w in (2 * half, 2 * half + 1):
                    mm = nc.tensor.matmul(dst[:], diag[:, i, w, :], upre[:, i % 2, w:w + T], start=(w == 0), stop=(w == 3))
                if half:
                    mm.then_inc(a_full, 1)

            def dbc_product(k, part):
                if part == 0:
                    fill_a()
                dst = bank_a[(a.n - 1) % 2]
                for i in (2 * part, 2 * part + 1):
                    pe.wait_ge(silu_u, k * CT + i + 1)
                    mm = nc.tensor.matmul(dst[:], wx[:, i, :], u[:, i, :], start=(i == 0), stop=(i == CT - 1))
                if part == 3:
                    mm.then_inc(a_full, 1)

            def c_turn():
                dst = fill_a()
                wait_a(a.value() - 1)
                for b in range(TB):
                    mm = nc.tensor.transpose(dst[:, b * P:(b + 1) * P], dbc[:, b * P:(b + 1) * P], ident[:])
                mm.then_inc(a_full, 1)

            def dt_product(i):
                dst = fill_a()
                nc.tensor.matmul(dst[:], wdt[:, i * P:(i + 1) * P], dbc[:], start=True, stop=True).then_inc(a_full, 1)

            def turn_h(k, g, r, b):
                n = g * STEPS + r
                if b == 0:
                    if r == 0:
                        pe.wait_ge(skip_ready, k * CT + (g + 1) * G)
                    else:
                        pe.wait_ge(scanned, k * UNITS + (g * NS + r) * G + SCAN_FREE)
                pe.wait_ge(t_free, k * T_PER + n * TB + b + 1)
                for q in range(G):
                    mm = nc.tensor.transpose(bank_t[b % 2][:, q * P:(q + 1) * P], hbuf[:, n % 2, q, b * P:(b + 1) * P], ident[:])
                mm.then_inc(t_full, 1)

            def turn_y(k, g, b):
                pe.wait_ge(t_free, k * T_PER + ((g + 1) * STEPS - 1) * TB + b + 1 + FREE)
                dst = fill_d()
                for q in range(G):
                    mm = nc.tensor.transpose(dst[:, q * P:(q + 1) * P], yT[:, b, q * P:(q + 1) * P], ident[:])
                mm.then_inc(d_full, 1)

            def out_product(g, b, after):
                if b % 2 == 0:
                    fill_d()
                dst = bank_d[(d.n - 1) % 2]
                gated = d.value() - b // 2 - 1 - (TB - 1 - b) - after
                pe.wait_ge(d_free, gated + FREE)
                for q in range(G):
                    mm = nc.tensor.matmul(dst[:, (b % 2) * C:(b % 2 + 1) * C], zs[:, q, b * P:(b + 1) * P], wout_c[:, g * G + q, :],
                                          start=(q == 0), stop=(q == G - 1))
                if b % 2:
                    mm.then_inc(d_full, 1)

            def beside(k, x, first, last, pre):
                if x in OUT_AT and not first:
                    out_product(1, OUT_AT.index(x), 0)
                if x in DT_HIGH_AT:
                    dt_product(G + DT_HIGH_AT.index(x))
                if x in Z_LOW_AT:
                    in_product(k, CT + Z_LOW_AT.index(x))
                if x in OUT_LOW_AT:
                    out_product(0, OUT_LOW_AT.index(x), 0)
                if x in Z_HIGH_AT:
                    in_product(k, CT + G + Z_HIGH_AT.index(x))
                if last:
                    return
                for v, at in enumerate(GNN_EARLY):
                    if x == at:
                        gnn_product(k + 1, NLATE + v)
                for v, at in enumerate(GNN_LATE):
                    if x == at and pre:
                        gnn_product(k + 2, v)
                if x in GT_AT:
                    gnn_turn(k + 1, GT_AT.index(x))
                if x in XLN_AT:
                    xln_turn(k + 1, XLN_AT.index(x))
                if x in IN_AT:
                    if x == IN_AT[0]:
                        wait_a(a.value())
                    in_product(k + 1, IN_AT.index(x))
                if x in CONV_AT:
                    conv(CONV_AT.index(x), 0)
                if x - 1 in CONV_AT:
                    conv(CONV_AT.index(x - 1), 1)
                if x in DBC_AT:
                    dbc_product(k + 1, DBC_AT.index(x))
                if x == C_AT:
                    c_turn()
                if x in DT_LOW_AT:
                    dt_product(DT_LOW_AT.index(x))

            def chunk(k, first=False, last=False, pre=True):
                for g in range(NG):
                    kp, gp = (k, 0) if g else (k - 1, 1)
                    for r in range(STEPS):
                        for b in range(TB):
                            if r == 0 and b < len(Y_AT) and (g or not first):
                                for block in Y_AT[b]:
                                    turn_y(kp, gp, block)
                            turn_h(k, g, r, b)
                            beside(k, (g * STEPS + r) * TB + b, first, last, pre)

            filler = iter(range(NLATE))

            def fill(count):
                for _ in range(count):
                    gnn_product(1, next(filler))

            for h in range(TB // 2):
                gnn_turn(0, h)
            fill(10)
            for f in range(FT):
                xln_turn(0, f)
            after_xln = a.value()
            fill(2)
            wait_a(after_xln)
            for i in range(CT):
                in_product(0, i)
                fill(2)
                for half in range(2):
                    conv(i, half)
            fill(4)
            for part in range(4):
                dbc_product(0, part)
            fill(2)
            c_turn()
            for i in range(G):
                dt_product(i)
                fill(2)
            fill(NLATE - 10 - 2 - 2 * CT - 4 - 2 - 2 * G)
            chunk(0, first=True)
            with pe.Fori(1, NCH - 2) as k:
                a.enter(k - 1)
                d.enter(k - 1)
                chunk(k)
                a.leave(NCH - 3)
                d.leave(NCH - 3)
            chunk(NCH - 2, pre=False)
            chunk(NCH - 1, last=True)
            for b in range(TB):
                turn_y(NCH - 1, 1, b)
            for b in range(TB):
                out_product(1, b, 0)

        @block.vector
        def _(dve):
            d = Tally(D_PER)
            me = Tally(2 * TB + TB // 2 + TB)

            def take():
                dve.wait_ge(d_full, d.next() + 1)
                return bank_d[(d.n - 1) % 2]

            dve.sem_inc(d_free, FREE)
            dve.sem_inc(t_free, FREE)
            dve.sem_inc(scanned, SCAN_FREE)
            dve.sem_inc(rows_free, 2)
            dve.wait_ge(act_const, 1)
            nc.vector.tensor_scalar(amat[:], amat[:], -1.0, None, ALU.mult).then_inc(dve_const, 1)
            dve.wait_ge(const_landed, CONST_ALL)
            dve.wait_ge(pool_const, 7)
            for i in range(CT):
                for w in range(4):
                    nc.vector.tensor_scalar(diag[:, i, w, :], ident[:], convw[:, i, w:w + 1], None, ALU.mult).then_inc(dve_const, 1)
            me.per = 2 * SETUP_SLOTS
            with dve.Fori(0, NJ // SETUP_SLOTS) as jp:
                me.enter(jp)
                for b in range(SETUP_SLOTS):
                    j = jp * SETUP_SLOTS + b
                    dve.wait_ge(rows_landed[b % 2], (jp * (SETUP_SLOTS // 2) + b // 2 + 1) * 16)
                    nc.vector.reduce_sum(stat[:, b, 0:1], rows[:, b % 2, :], AX_X).then_inc(rows_free, 1)
                    dve.wait_ge(rows_free, j + 3)
                    dve.wait_ge(xj_landed[b], (jp + 1) * 16)
                    nc.vector.bn_stats(st[:, b, :], xj[:, b, :]).then_inc(dve_self, 1)
                    dve.wait_ge(dve_self, me.next())
                    nc.vector.tensor_scalar(stat[:, b, 0:1], stat[:, b, 0:1], 1.0, None, ALU.add)
                    nc.vector.bn_aggr(mv[:, b, :], st[:, b, :]).then_inc(dve_self, 1)
                    dve.wait_ge(dve_self, me.next())
                    nc.vector.tensor_scalar(stat[:, b, 1:2], mv[:, b, 1:2], EPS, None, ALU.add).then_inc(stat_ready, 1)
                    dve.wait_ge(pow_done, j + 1)
                    nc.vector.tensor_scalar(xj[:, b, :], xj[:, b, :], mv[:, b, 0:1], srstd[:, b:b + 1],
                                            ALU.subtract, ALU.mult).then_inc(xn_ready, 1)
                me.leave(NJ // SETUP_SLOTS)
            me.per = 2 * TB + TB // 2 + TB

            def x1_part(k, h, part):
                pair = slice(2 * h, 2 * h + 2)
                if part == 0:
                    if h == 0:
                        dve.wait_ge(x_landed, (k + 1) * 32)
                    src = take()
                    nc.vector.tensor_tensor(x1[:, pair, :], src[:].rearrange("p (b c) -> p b c", b=2), xwi[:, pair, :],
                                            ALU.add).then_inc(d_free, 1)
                if part == 1:
                    dve.wait_ge(d_free, d.value() + FREE)
                    for b in range(2 * h, 2 * h + 2):
                        nc.vector.scalar_tensor_tensor(x1[:, b, :], x1[:, b, :], dinv[:, bass.ds(k * TB + b, 1)], gnn_b[:],
                                                       ALU.mult, ALU.add).then_inc(dve_self, 1)
                        me.next()
                if part == 2:
                    dve.wait_ge(dve_self, me.value())
                    nc.vector.scalar_tensor_tensor(x1[:, pair, :], x1[:, pair, :], 0.0, xin[:, pair, :],
                                                   ALU.max, ALU.add).then_inc(dve_self, 1)
                    me.next()
                if part == 3:
                    dve.wait_ge(dve_self, me.value())
                    for b in range(2 * h, 2 * h + 2):
                        nc.vector.bn_stats(st[:, b, :], x1[:, b, :]).then_inc(dve_self, 1)
                        if b:
                            nc.vector.bn_aggr(mv[:, b - 1, :], st[:, b - 1, :]).then_inc(dve_self, 1)
                            me.next()
                        dve.wait_ge(dve_self, me.next())

            def variance():
                last = TB - 1
                nc.vector.tensor_scalar(mv[:, 0:last, 1], mv[:, 0:last, 1], EPS, None, ALU.add)
                nc.vector.bn_aggr(mv[:, last, :], st[:, last, :]).then_inc(dve_self, 1)
                dve.wait_ge(dve_self, me.next())
                nc.vector.tensor_scalar(mv[:, last, 1:2], mv[:, last, 1:2], EPS, None, ALU.add).then_inc(var_ready, 1)

            def xln(k):
                dve.wait_ge(rstd_ready, k + 1)
                for b in range(TB):
                    nc.vector.tensor_scalar(xin[:, b, :], x1[:, b, :], mv[:, b, 0:1], rstd[:, b:b + 1],
                                            ALU.subtract, ALU.mult).then_inc(xln_ready, 1)

            def scan(k, g, s, q):
                unit = (g * NS + s) * G + q
                n = g * STEPS + s + 1
                if q == 0:
                    dve.wait_ge(t_full, k * T_PER + n * TB)
                    dve.wait_ge(saved, (k + 1) * (NG * NS) + g * NS + max(s - 1, 0))
                dve.wait_ge(decay_ready, k * UNITS + unit + 1)
                dve.wait_ge(drive_ready, k * UNITS + unit + 1 + DRIVE_FREE)
                nc.vector.tensor_tensor_scan(hbuf[:, n % 2, q, :], decay[:, unit % DEC_SLOTS, :], drive[:, unit % DRV_SLOTS, :],
                                             state[:, s, g * G + q:g * G + q + 1], ALU.mult, ALU.add).then_inc(scanned, 1)

            def add_up(k, g, r, b):
                use = k * T_PER + (g * STEPS + r) * TB + b
                dve.wait_ge(t_full, use + 1 + TB)
                dve.wait_ge(t_free, use + FREE if r == 1 and b == 0 else use - TB + 1 + FREE)
                nc.vector.scalar_tensor_tensor(yT[:, b, :], bank_t[b % 2][:], ccol[:, bass.ds(k * TB + b, 1), r - 1],
                                               yT[:, b, :], ALU.mult, ALU.add).then_inc(t_free, 1)

            def gate(k, g, b):
                if b == 0:
                    dve.wait_ge(silu_z, k * CT + (g + 1) * G)
                src = take()
                part = zs[:, :, b * P:(b + 1) * P]
                nc.vector.tensor_tensor(part, src[:].rearrange("p (q t) -> p q t", q=G), part, ALU.mult).then_inc(d_free, 1)

            def add_out(k, h):
                if h == 0:
                    dve.wait_ge(xo_ready, (k + 1) * TB)
                src = take()
                pair = slice(2 * h, 2 * h + 2)
                acc = xo[:, bass.ds(k % 2, 1), pair, :].rearrange("p o b c -> p (o b) c")
                nc.vector.tensor_tensor(acc, src[:].rearrange("p (b c) -> p b c", b=2), acc, ALU.add).then_inc(d_free, 1)

            def beside(k, x, first, last):
                for h in range(TB // 2):
                    if x == OUT_AT[2 * h + 1] + 5 and not first:
                        add_out(k - 1, h)
                    if x == OUT_LOW_AT[2 * h + 1] + 5:
                        add_out(k, h)
                if x in X1_AT and not last:
                    i = X1_AT.index(x)
                    if i == 0:
                        dve.wait_ge(xo_ready, (k + 1) * TB)
                    x1_part(k + 1, i // 4, i % 4)
                    if i == len(X1_AT) - 1:
                        variance()
                if x == LN_AT and not last:
                    xln(k + 1)

            def chunk(k, first=False, last=False):
                dve.wait_ge(c_ready, k + 1)
                for g in range(NG):
                    kp, gp = (k, 0) if g else (k - 1, 1)
                    if g or not first:
                        for b in range(TB):
                            add_up(kp, gp, NS, b)
                    for q in range(G):
                        scan(k, g, 0, q)
                        if g or not first:
                            gate(kp, gp, q)
                    for s in range(1, NS):
                        for q in range(G):
                            scan(k, g, s, q)
                            add_up(k, g, s, q)
                            beside(k, (g * STEPS + s + 1) * TB + q, first, last)

            for h in range(TB // 2):
                for part in range(4):
                    x1_part(0, h, part)
            variance()
            xln(0)
            chunk(0, first=True)
            with dve.Fori(1, NCH - 2) as k:
                d.enter(k - 1)
                me.enter(k - 1)
                chunk(k)
                d.leave(NCH - 3)
                me.leave(NCH - 3)
            chunk(NCH - 2)
            chunk(NCH - 1, last=True)
            for b in range(TB):
                add_up(NCH - 1, 1, NS, b)
            for b in range(TB):
                gate(NCH - 1, 1, b)
            for h in range(TB // 2):
                add_out(NCH - 1, h)


INPUTS = ("adj", "adjT", "x", "gnn_w", "gnn_b", "wfc1", "bfc1", "winT", "conv_w", "conv_b", "wxT", "wdtT", "b_dt",
          "A_log", "D", "wout", "wfc2T", "b_fc2")


def kernel(x, adj, L0_gnn_W, L0_gnn_b, L0_ffn_W_fc1, L0_ffn_b_fc1, L0_ffn_W_in, L0_ffn_conv_w, L0_ffn_conv_b,
           L0_ffn_W_xproj, L0_ffn_W_dt, L0_ffn_b_dt, L0_ffn_A_log, L0_ffn_D, L0_ffn_W_out, L0_ffn_W_fc2, L0_ffn_b_fc2):
    import concourse.bacc as bacc
    from concourse.bass_utils import run_bass_kernel_spmd

    def by_channel(v):
        v = np.asarray(v)
        w = v.reshape(v.shape[0] // P, P, -1).transpose(1, 0, 2)
        return w if v.ndim > 1 else w[:, :, 0]

    arrays = dict(
        adj=adj, adjT=np.asarray(adj).T, x=x, gnn_w=np.asarray(L0_gnn_W).T, gnn_b=L0_gnn_b, wfc1=L0_ffn_W_fc1,
        bfc1=by_channel(L0_ffn_b_fc1), winT=np.asarray(L0_ffn_W_in).T, conv_w=by_channel(L0_ffn_conv_w),
        conv_b=by_channel(L0_ffn_conv_b), wxT=np.asarray(L0_ffn_W_xproj).T, wdtT=np.asarray(L0_ffn_W_dt).T,
        b_dt=by_channel(L0_ffn_b_dt), A_log=by_channel(L0_ffn_A_log), D=by_channel(L0_ffn_D), wout=L0_ffn_W_out,
        wfc2T=np.asarray(L0_ffn_W_fc2).T, b_fc2=L0_ffn_b_fc2)
    arrays = {"in_" + n: np.ascontiguousarray(arrays[n]) for n in INPUTS}
    nc = bacc.Bacc("TRN2", target_bir_lowering=False, num_devices=1)
    t = {n: nc.dram_tensor("in_" + n, arrays["in_" + n].shape, F32, kind="ExternalInput").ap() for n in INPUTS}
    t["out"] = nc.dram_tensor("out", [N, C], F32, kind="ExternalOutput").ap()
    build(nc, t)
    return run_bass_kernel_spmd(nc, [arrays], core_ids=[0]).results[0]["out"]
```
